# Optimizing a Trainium2 kernel written in Bass

```python
import numpy as np
import jax
import jax.numpy as jnp

def _softmax(x, axis=-1):
    return jax.nn.softmax(x, axis=axis)

def _gelu(x):
    return jax.nn.gelu(x, approximate=True)

def _silu(x):
    return jax.nn.silu(x)

def _sigmoid(x):
    return jax.nn.sigmoid(x)

def _layernorm(x, axis=-1, eps=1e-05):
    m = jnp.mean(x, axis=axis, keepdims=True)
    v = jnp.var(x, axis=axis, keepdims=True)
    return (x - m) / jnp.sqrt(v + eps)

def _scatter_add(tgt, idx, src, axis=0):
    return tgt.at[idx].add(src)

def _segment_sum(src, seg, n):
    return jax.ops.segment_sum(src, seg, n)
kernel_name = 'mk_adaln_d1_jaxref_r4_d3448b'

def setup_inputs(seed: int=0):
    np.random.seed(seed)
    _w = jnp.asarray

    def _L0_attn_setup():
        import jax, jax.numpy as jnp
        import numpy as np
        D_MODEL = 256
        D_INNER = 512
        D_STATE = 16
        D_CONV = 4
        DT_RANK = 64
        BATCH = 2
        SEQ = 256
        LN_EPS = 1e-05

        def _mk_layer(key):
            k = jax.random.split(key, 5)
            return {'in_proj': jax.random.normal(k[0], (2 * D_INNER, D_MODEL)) * 0.02, 'conv_w': jax.random.normal(k[1], (D_INNER, 1, D_CONV)) * 0.2, 'conv_b': jnp.zeros((D_INNER,)), 'x_proj': jax.random.normal(k[2], (DT_RANK + 2 * D_STATE, D_INNER)) * 0.02, 'dt_w': jax.random.normal(k[3], (D_INNER, DT_RANK)) * 0.02, 'dt_b': jnp.full((D_INNER,), -4.6), 'A_log': jnp.log(jnp.tile(jnp.arange(1.0, D_STATE + 1.0), (D_INNER, 1))), 'D': jnp.ones((D_INNER,)), 'out_proj': jax.random.normal(k[4], (D_MODEL, D_INNER)) * 0.02}

        def _mamba(x, in_proj, conv_w, conv_b, x_proj, dt_w, dt_b, A_log, Dp, out_proj):
            Bb, L, _ = x.shape
            xz = jnp.einsum('bld,ed->ble', x, in_proj)
            xi, z = jnp.split(xz, 2, axis=-1)
            xc = jnp.transpose(xi, (0, 2, 1))
            xc = jax.lax.conv_general_dilated(xc, conv_w, (1,), [(D_CONV - 1, 0)], dimension_numbers=('NCH', 'OIH', 'NCH'), feature_group_count=D_INNER)
            xc = xc + conv_b[None, :, None]
            xi = jax.nn.silu(jnp.transpose(xc, (0, 2, 1)))
            dbc = jnp.einsum('bld,ed->ble', xi, x_proj)
            dt, Bm, Cm = jnp.split(dbc, [DT_RANK, DT_RANK + D_STATE], axis=-1)
            dt = jax.nn.softplus(jnp.einsum('blr,dr->bld', dt, dt_w) + dt_b)
            A = -jnp.exp(A_log)
            dA = jnp.exp(dt[..., None] * A)
            dBx = (dt * xi)[..., None] * Bm[:, :, None, :]

            def step(h, inp):
                a, bx, c = inp
                h = a * h + bx
                return (h, jnp.einsum('bds,bs->bd', h, c))
            h0 = jnp.zeros((Bb, D_INNER, D_STATE), x.dtype)
            _, ys = jax.lax.scan(step, h0, (jnp.moveaxis(dA, 1, 0), jnp.moveaxis(dBx, 1, 0), jnp.moveaxis(Cm, 1, 0)))
            y = jnp.moveaxis(ys, 0, 1) + xi * Dp
            y = y * jax.nn.silu(z)
            return jnp.einsum('ble,de->bld', y, out_proj)
        key = jax.random.key(seed)
        kx, kf, kb = jax.random.split(key, 3)
        inp = {'x': jax.random.normal(kx, (BATCH, SEQ, D_MODEL), jnp.float32)}
        for pref, kk in (('f_', kf), ('b_', kb)):
            for name, v in _mk_layer(kk).items():
                inp[pref + name] = v
        inp['ln_g'] = jnp.ones((D_MODEL,))
        inp['ln_b'] = jnp.zeros((D_MODEL,))
        return inp
    _L0_attn_in = _L0_attn_setup()

    def _L0_ffn_setup():
        import jax, jax.numpy as jnp
        import numpy as np
        D_IN, D_HID = (256, 1024)

        def _ternary(key, shape):
            return jax.random.randint(key, shape, -1, 2).astype(jnp.float32)

        def _tlin(x, w, s):
            return jnp.einsum('bsi,oi->bso', x, w) * s
        key = jax.random.key(seed)
        ks = jax.random.split(key, 12)
        inv = lambda fan: 1.0 / np.sqrt(fan).astype(np.float32)
        return {'x': jax.random.normal(ks[0], (4, 512, D_IN), dtype=jnp.float32), 'w1_w': _ternary(ks[1], (D_HID, D_IN)), 'w1_s': jax.random.uniform(ks[2], (D_HID,), dtype=jnp.float32) * inv(D_IN), 'w2_w': _ternary(ks[3], (D_HID, D_IN)), 'w2_s': jax.random.uniform(ks[4], (D_HID,), dtype=jnp.float32) * inv(D_IN), 'h1_w': _ternary(ks[5], (D_HID, D_HID)), 'h1_s': jax.random.uniform(ks[6], (D_HID,), dtype=jnp.float32) * inv(D_HID), 'h2_w': _ternary(ks[7], (D_HID, D_HID)), 'h2_s': jax.random.uniform(ks[8], (D_HID,), dtype=jnp.float32) * inv(D_HID), 'w3_w': _ternary(ks[9], (D_IN, D_HID)), 'w3_s': jax.random.uniform(ks[10], (D_IN,), dtype=jnp.float32) * inv(D_HID)}
    _L0_ffn_in = _L0_ffn_setup()
    _L0_c = _w((lambda *s: np.random.randn(*s).astype(np.float32) * 0.05)(2, 256))
    _L0_wmod = _w((lambda *s: np.random.randn(*s).astype(np.float32) * 0.05)(256, 6 * 256) * 256 ** (-0.5))
    _d = {'L0_attn_x': _L0_attn_in['x'], 'L0_attn_f_in_proj': _L0_attn_in['f_in_proj'], 'L0_attn_f_conv_w': _L0_attn_in['f_conv_w'], 'L0_attn_f_conv_b': _L0_attn_in['f_conv_b'], 'L0_attn_f_x_proj': _L0_attn_in['f_x_proj'], 'L0_attn_f_dt_w': _L0_attn_in['f_dt_w'], 'L0_attn_f_dt_b': _L0_attn_in['f_dt_b'], 'L0_attn_f_A_log': _L0_attn_in['f_A_log'], 'L0_attn_f_D': _L0_attn_in['f_D'], 'L0_attn_f_out_proj': _L0_attn_in['f_out_proj'], 'L0_attn_b_in_proj': _L0_attn_in['b_in_proj'], 'L0_attn_b_conv_w': _L0_attn_in['b_conv_w'], 'L0_attn_b_conv_b': _L0_attn_in['b_conv_b'], 'L0_attn_b_x_proj': _L0_attn_in['b_x_proj'], 'L0_attn_b_dt_w': _L0_attn_in['b_dt_w'], 'L0_attn_b_dt_b': _L0_attn_in['b_dt_b'], 'L0_attn_b_A_log': _L0_attn_in['b_A_log'], 'L0_attn_b_D': _L0_attn_in['b_D'], 'L0_attn_b_out_proj': _L0_attn_in['b_out_proj'], 'L0_attn_ln_g': _L0_attn_in['ln_g'], 'L0_attn_ln_b': _L0_attn_in['ln_b'], 'L0_ffn_w1_w': _L0_ffn_in['w1_w'], 'L0_ffn_w1_s': _L0_ffn_in['w1_s'], 'L0_ffn_w2_w': _L0_ffn_in['w2_w'], 'L0_ffn_w2_s': _L0_ffn_in['w2_s'], 'L0_ffn_h1_w': _L0_ffn_in['h1_w'], 'L0_ffn_h1_s': _L0_ffn_in['h1_s'], 'L0_ffn_h2_w': _L0_ffn_in['h2_w'], 'L0_ffn_h2_s': _L0_ffn_in['h2_s'], 'L0_ffn_w3_w': _L0_ffn_in['w3_w'], 'L0_ffn_w3_s': _L0_ffn_in['w3_s'], 'L0_c': _L0_c, 'L0_wmod': _L0_wmod}
    _x0 = _d['L0_attn_x']
    _d['L0_attn_x'] = jax.random.normal(jax.random.fold_in(jax.random.key(seed), 1), (2, 4096, 256), dtype=_x0.dtype)
    del _x0
    return _d

def reference(L0_attn_x, L0_attn_f_in_proj, L0_attn_f_conv_w, L0_attn_f_conv_b, L0_attn_f_x_proj, L0_attn_f_dt_w, L0_attn_f_dt_b, L0_attn_f_A_log, L0_attn_f_D, L0_attn_f_out_proj, L0_attn_b_in_proj, L0_attn_b_conv_w, L0_attn_b_conv_b, L0_attn_b_x_proj, L0_attn_b_dt_w, L0_attn_b_dt_b, L0_attn_b_A_log, L0_attn_b_D, L0_attn_b_out_proj, L0_attn_ln_g, L0_attn_ln_b, L0_ffn_w1_w, L0_ffn_w1_s, L0_ffn_w2_w, L0_ffn_w2_s, L0_ffn_h1_w, L0_ffn_h1_s, L0_ffn_h2_w, L0_ffn_h2_s, L0_ffn_w3_w, L0_ffn_w3_s, L0_c, L0_wmod):

    def _L0_attn_ref(x, f_in_proj, f_conv_w, f_conv_b, f_x_proj, f_dt_w, f_dt_b, f_A_log, f_D, f_out_proj, b_in_proj, b_conv_w, b_conv_b, b_x_proj, b_dt_w, b_dt_b, b_A_log, b_D, b_out_proj, ln_g, ln_b):
        import jax, jax.numpy as jnp
        import numpy as np
        D_MODEL = 256
        D_INNER = 512
        D_STATE = 16
        D_CONV = 4
        DT_RANK = 64
        BATCH = 2
        SEQ = 256
        LN_EPS = 1e-05

        def _mk_layer(key):
            k = jax.random.split(key, 5)
            return {'in_proj': jax.random.normal(k[0], (2 * D_INNER, D_MODEL)) * 0.02, 'conv_w': jax.random.normal(k[1], (D_INNER, 1, D_CONV)) * 0.2, 'conv_b': jnp.zeros((D_INNER,)), 'x_proj': jax.random.normal(k[2], (DT_RANK + 2 * D_STATE, D_INNER)) * 0.02, 'dt_w': jax.random.normal(k[3], (D_INNER, DT_RANK)) * 0.02, 'dt_b': jnp.full((D_INNER,), -4.6), 'A_log': jnp.log(jnp.tile(jnp.arange(1.0, D_STATE + 1.0), (D_INNER, 1))), 'D': jnp.ones((D_INNER,)), 'out_proj': jax.random.normal(k[4], (D_MODEL, D_INNER)) * 0.02}

        def _mamba(x, in_proj, conv_w, conv_b, x_proj, dt_w, dt_b, A_log, Dp, out_proj):
            Bb, L, _ = x.shape
            xz = jnp.einsum('bld,ed->ble', x, in_proj)
            xi, z = jnp.split(xz, 2, axis=-1)
            xc = jnp.transpose(xi, (0, 2, 1))
            xc = jax.lax.conv_general_dilated(xc, conv_w, (1,), [(D_CONV - 1, 0)], dimension_numbers=('NCH', 'OIH', 'NCH'), feature_group_count=D_INNER)
            xc = xc + conv_b[None, :, None]
            xi = jax.nn.silu(jnp.transpose(xc, (0, 2, 1)))
            dbc = jnp.einsum('bld,ed->ble', xi, x_proj)
            dt, Bm, Cm = jnp.split(dbc, [DT_RANK, DT_RANK + D_STATE], axis=-1)
            dt = jax.nn.softplus(jnp.einsum('blr,dr->bld', dt, dt_w) + dt_b)
            A = -jnp.exp(A_log)
            dA = jnp.exp(dt[..., None] * A)
            dBx = (dt * xi)[..., None] * Bm[:, :, None, :]

            def step(h, inp):
                a, bx, c = inp
                h = a * h + bx
                return (h, jnp.einsum('bds,bs->bd', h, c))
            h0 = jnp.zeros((Bb, D_INNER, D_STATE), x.dtype)
            _, ys = jax.lax.scan(step, h0, (jnp.moveaxis(dA, 1, 0), jnp.moveaxis(dBx, 1, 0), jnp.moveaxis(Cm, 1, 0)))
            y = jnp.moveaxis(ys, 0, 1) + xi * Dp
            y = y * jax.nn.silu(z)
            return jnp.einsum('ble,de->bld', y, out_proj)
        xb = x[:, ::-1, :]
        yf = jax.nn.sigmoid(_mamba(x, f_in_proj, f_conv_w, f_conv_b, f_x_proj, f_dt_w, f_dt_b, f_A_log, f_D, f_out_proj))
        yb = jax.nn.sigmoid(_mamba(xb, b_in_proj, b_conv_w, b_conv_b, b_x_proj, b_dt_w, b_dt_b, b_A_log, b_D, b_out_proj))
        d = 0.5 * (yf + yb[:, ::-1, :])
        mu = jnp.mean(d, axis=-1, keepdims=True)
        var = jnp.var(d, axis=-1, keepdims=True)
        d = (d - mu) * jax.lax.rsqrt(var + LN_EPS) * ln_g + ln_b
        return d + x

    def _L0_ffn_ref(x, w1_w, w1_s, w2_w, w2_s, h1_w, h1_s, h2_w, h2_s, w3_w, w3_s):
        import jax, jax.numpy as jnp
        import numpy as np
        D_IN, D_HID = (256, 1024)

        def _ternary(key, shape):
            return jax.random.randint(key, shape, -1, 2).astype(jnp.float32)

        def _tlin(x, w, s):
            return jnp.einsum('bsi,oi->bso', x, w) * s
        h = jax.nn.silu(_tlin(x, w1_w, w1_s)) * _tlin(x, w2_w, w2_s)
        h = jax.nn.gelu(_tlin(h, h1_w, h1_s), approximate=False)
        h = jax.nn.gelu(_tlin(h, h2_w, h2_s), approximate=False)
        return _tlin(h, w3_w, w3_s)
    x = L0_attn_x
    mod = (_silu(L0_c) @ L0_wmod).reshape(L0_c.shape[0], 6, 1, -1)
    sa, ca, ga, sb, cb, gb = (mod[:, 0], mod[:, 1], mod[:, 2], mod[:, 3], mod[:, 4], mod[:, 5])
    ga = (2 * (ga >= 0) - 1) * jnp.maximum(jnp.abs(ga), 0.25)
    gb = (2 * (gb >= 0) - 1) * jnp.maximum(jnp.abs(gb), 0.25)
    h = _layernorm(x, axis=-1) * (1 + ca) + sa
    x = x + ga * _L0_attn_ref(h, L0_attn_f_in_proj, L0_attn_f_conv_w, L0_attn_f_conv_b, L0_attn_f_x_proj, L0_attn_f_dt_w, L0_attn_f_dt_b, L0_attn_f_A_log, L0_attn_f_D, L0_attn_f_out_proj, L0_attn_b_in_proj, L0_attn_b_conv_w, L0_attn_b_conv_b, L0_attn_b_x_proj, L0_attn_b_dt_w, L0_attn_b_dt_b, L0_attn_b_A_log, L0_attn_b_D, L0_attn_b_out_proj, L0_attn_ln_g, L0_attn_ln_b)
    h = _layernorm(x, axis=-1) * (1 + cb) + sb
    x = x + gb * _L0_ffn_ref(h, L0_ffn_w1_w, L0_ffn_w1_s, L0_ffn_w2_w, L0_ffn_w2_s, L0_ffn_h1_w, L0_ffn_h1_s, L0_ffn_h2_w, L0_ffn_h2_s, L0_ffn_w3_w, L0_ffn_w3_s)
    return x

_drawn_inputs = setup_inputs


def setup_inputs(seed=0):
    import zlib

    import numpy as np

    out = dict(_drawn_inputs(seed))
    spreads = {'L0_attn_f_conv_b': (0.0, 0.1),
     'L0_attn_f_dt_b': (-4.599999904632568, 0.2),
     'L0_attn_f_D': (1.0, 0.2),
     'L0_attn_b_conv_b': (0.0, 0.1),
     'L0_attn_b_dt_b': (-4.599999904632568, 0.2),
     'L0_attn_b_D': (1.0, 0.2),
     'L0_attn_ln_g': (1.0, 0.2),
     'L0_attn_ln_b': (0.0, 0.1)}
    factors = {}
    for name, (base, spread) in spreads.items():
        noise = np.random.default_rng([zlib.crc32(name.encode()), seed]).standard_normal(out[name].shape)
        drawn = base * np.exp(spread * noise) if base else spread * noise
        out[name] = jnp.asarray(drawn.astype(out[name].dtype))
    for name, factor in factors.items():
        out[name] = (out[name] * factor).astype(out[name].dtype)
    return out
```

```python
from contextlib import ExitStack

import concourse.bass as bass
from concourse import mybir

F32 = mybir.dt.float32
ALU = mybir.AluOpType
ACT = mybir.ActivationFunctionType

P = 128
BATCH, SEQ, DM = 2, 4096, 256
DI, DS, DCONV, DTR, DH = 512, 16, 4, 64, 1024
LNK = 6
T = 512
NC = SEQ // T
NCH = BATCH * NC
TS = T // P
KM = DM // P
KI = DI // P
KH = DH // P
HALO = DCONV - 1
B0 = DTR
STEPS = DS * KI
EPS = 1e-5
EXP_CAP = 2.0 ** 60

COL_CW, COL_CB, COL_DTB, COL_D, COL_A = 0, 16, 20, 24, 28
NCOL = COL_A + KI * DS

J_Y, J_OUT, J_LN, J_X, J_CONV, J_Z, J_B, J_C, J_DT, JOBS = 0, 4, 6, 8, 12, 16, 20, 21, 22, 26
FRONT_JOBS, TAIL_JOBS = JOBS - J_LN, J_LN
PASS_JOBS = NCH * JOBS


class Chunk:

    def __init__(self, ps, c, d):
        self.ps, self.c, self.d = ps, c, d
        self.batch = d % BATCH
        self.step = c + d // BATCH if isinstance(c, int) else c + (d // BATCH)

    def go(self, k):
        return Chunk(self.ps, self.c, self.d + k)

    def number(self):
        return BATCH * self.c + self.d if isinstance(self.c, int) else None

    def first(self):
        return self.number() == 0

    def last(self):
        return self.number() == NCH - 1

    def at(self, per_chunk, off):
        return self.c * (BATCH * per_chunk) + (per_chunk * (NCH * self.ps + self.d) + off)

    def time(self, reverse):
        k = self.d // BATCH
        return (self.c * -1) + (NC - 1 - k) if reverse else self.c + k


def wait(eng, sem, value):
    if not (isinstance(value, int) and value <= 0):
        eng.wait_ge(sem, value)


def adaln_mamba_ffn(nc, a, out, yb_dram, x1_dram):
    x_v = a["x"].rearrange("b (c s p) d -> b c p s d", s=TS, p=P)
    yb_v = yb_dram.rearrange("b (c s p) d -> b c p s d", s=TS, p=P)
    x1_v = x1_dram.rearrange("b (c s p) d -> b c p s d", s=TS, p=P)
    out_v = out.rearrange("b (c s p) d -> b c p s d", s=TS, p=P)

    with ExitStack() as ctx:
        def sem(name):
            return ctx.enter_context(nc.semaphore(name))

        def sbuf(c, name, shape, dt=F32):
            return c.enter_context(nc.sbuf_tensor(name, shape, dt))

        bank = [ctx.enter_context(nc.psum_tensor(f"bank{i}", [P, T], F32)) for i in range(8)]

        ident = sbuf(ctx, "ident", [P, P])
        sel = sbuf(ctx, "sel", [P, DS, P])
        cols = sbuf(ctx, "cols", [P, 2, NCOL])
        mod = sbuf(ctx, "mod", [P, 12, BATCH])
        gain = sbuf(ctx, "gain", [P, 4, BATCH, DM])
        norm_c = sbuf(ctx, "norm_c", [P, 2, TS])
        fcol = sbuf(ctx, "fcol", [P, 4, KH])

        setup(nc, ctx, sem, sbuf, a, bank, ident, sel, cols, mod, gain, norm_c, fcol)
        S = {n: sem(n) for n in SEM_NAMES}
        for ps in range(2):
            mamba_pass(nc, ps, a, bank, ident, sel, cols, mod, gain, norm_c, x_v, yb_v, x1_v, S)
        ffn(nc, sem, sbuf, a, bank, ident, mod, gain, norm_c, fcol, x1_v, out_v)


SEM_NAMES = [
    "w_in", "init", "go", "x_in", "ln", "fill0", "fill1", "drain0", "drain1", "halo", "exp1", "cap", "lnp",
    "u_ready", "b_fill", "b_copied", "da", "dbx", "scan", "save", "ht_fill", "stt", "gate", "y_out", "yb_in",
    "xr_in", "comb",
]


def setup(nc, ctx, sem, sbuf, a, bank, ident, sel, cols, mod, gain, norm_c, fcol):
    with ExitStack() as c:
        ct = sbuf(c, "ct", [P, KM, BATCH])
        cs = sbuf(c, "cs", [P, KM, BATCH])
        cbc = sbuf(c, "cbc", [P, KM, BATCH, P])
        wmod = sbuf(c, "wmod", [P, KM, 6 * DM])
        lng = sbuf(c, "lng", [P, 3, DM])
        rows = sbuf(c, "rows", [P, BATCH, 6, DM])
        ones = sbuf(c, "ones", [P, P])
        sgn = sbuf(c, "sgn", [P, BATCH, DM])
        mag = sbuf(c, "mag", [P, BATCH, DM])
        t0 = sbuf(c, "t0", [P, BATCH, DM])
        s_in, s_pool, s_silu, s_v, s_pe, s_a = (c.enter_context(nc.semaphore(n)) for n in
                                                ("s_in", "s_pool", "s_silu", "s_v", "s_pe", "s_a"))
        block = c.enter_context(nc.Block())

        @block.sync
        def _(sp):
            sp.dma_start(ct[:, :, :], a["cT"].rearrange("(k p) b -> p k b", p=P)).then_inc(s_in, 16)
            sp.dma_start(wmod[:, :, :], a["wmod"].rearrange("(k p) n -> p k n", p=P)).then_inc(s_in, 16)
            sp.dma_start(cols[:, 0, :], a["b_cols"]).then_inc(s_in, 16)
            sp.dma_start(cols[:, 1, :], a["f_cols"]).then_inc(s_in, 16)
            sp.dma_start(fcol[:, :, :], a["ffn_cols"]).then_inc(s_in, 16)
            for i, name in enumerate(("ln_g", "ln_b", "w3_s")):
                sp.dma_start(lng[:, i, :], a[name].partition_broadcast(P)).then_inc(s_in, 16)

        @block.gpsimd
        def _(pool):
            pool.memset(ident[:, :], 0.0).then_inc(s_pool, 1)
            pool.memset(sel[:, :, :], 0.0).then_inc(s_pool, 1)
            pool.memset(norm_c[:, 0, :], EPS)
            pool.memset(norm_c[:, 1, :], -0.5)
            pool.memset(ones[:, :], 1.0).then_inc(s_pool, 1)
            pool.wait_ge(s_pool, 3)
            pool.affine_select(out=ident[:, :], in_=ident[:, :], compare_op=ALU.not_equal, fill=1.0, base=0,
                               pattern=[[-1, P]], channel_multiplier=1).then_inc(s_pool, 1)
            pool.affine_select(out=sel[:, :, :], in_=sel[:, :, :], compare_op=ALU.not_equal, fill=1.0, base=-B0,
                               pattern=[[-1, DS], [0, P]], channel_multiplier=1).then_inc(s_pool, 1)

        @block.scalar
        def _(act):
            act.wait_ge(s_in, 128)
            act.activation(cs[:, :, :], ct[:, :, :], ACT.Silu).then_inc(s_silu, 1)
            for d in range(2):
                act.activation(cols[:, d, COL_A:], cols[:, d, COL_A:], ACT.Exp).then_inc(s_a, 1)

        @block.tensor
        def _(pe):
            pe.wait_ge(s_silu, 1)
            for j in range(12):
                for k in range(KM):
                    last = pe.matmul(bank[0][:, 2 * j:2 * j + 2], wmod[:, k, j * P:(j + 1) * P], cs[:, k, :],
                                     start=(k == 0), stop=(k == KM - 1))
            last.then_inc(s_pe, 1)
            pe.wait_ge(s_v, 1)
            for b in range(BATCH):
                for j in range(3):
                    for k in range(KM):
                        last = pe.matmul(bank[1 + 3 * b + j][:, :], cbc[:, k, b, :],
                                         wmod[:, k, 2 * j * DM:2 * (j + 1) * DM], start=(k == 0), stop=(k == KM - 1))
            last.then_inc(s_pe, 1)

        @block.vector
        def _(dve):
            n = [0]

            def step(ins):
                n[0] += 1
                ins.then_inc(s_v, 1)
                dve.wait_ge(s_v, n[0])

            dve.wait_ge(s_silu, 1)
            dve.wait_ge(s_pool, 3)
            for k in range(KM):
                for b in range(BATCH):
                    last = dve.tensor_scalar(cbc[:, k, b, :], ones[:, :], cs[:, k, b:b + 1], None, ALU.mult)
            step(last)
            dve.wait_ge(s_a, 2)
            step(dve.tensor_scalar(cols[:, :, COL_A:], cols[:, :, COL_A:], -1.0, None, ALU.mult))
            dve.wait_ge(s_pe, 1)
            step(dve.tensor_copy(mod[:, :, :], bank[0][:, 0:24].rearrange("p (j b) -> p j b", b=BATCH)))
            for part in (1, 4):
                m = mod[:, 2 * part:2 * part + 2, :]
                step(dve.tensor_scalar(m, m, 1.0, None, ALU.add))
            dve.wait_ge(s_pe, 2)
            for b in range(BATCH):
                for j in range(3):
                    step(dve.tensor_copy(rows[:, b, 2 * j:2 * j + 2, :],
                                         bank[1 + 3 * b + j][:, :].rearrange("p (g n) -> p g n", g=2)))
            for part in (2, 5):
                g = rows[:, :, part, :]
                step(dve.tensor_scalar(sgn[:, :, :], g, 0.0, 2.0, ALU.is_ge, ALU.mult))
                step(dve.tensor_scalar(sgn[:, :, :], sgn[:, :, :], -1.0, None, ALU.add))
                step(dve.tensor_scalar(mag[:, :, :], g, -1.0, 0.25, ALU.mult, ALU.max))
                step(dve.tensor_tensor(mag[:, :, :], mag[:, :, :], g, ALU.max))
                step(dve.tensor_tensor(g, sgn[:, :, :], mag[:, :, :], ALU.mult))
            for b in range(BATCH):
                ga, gb = rows[:, b, 2, :], rows[:, b, 5, :]
                step(dve.scalar_tensor_tensor(out=gain[:, 0, b, :], in0=ga, scalar=0.5, in1=lng[:, 0, :],
                                              op0=ALU.mult, op1=ALU.mult))
                step(dve.tensor_scalar(t0[:, b, :], rows[:, b, 1, :], 1.0, None, ALU.add))
                step(dve.tensor_tensor(gain[:, 1, b, :], ga, t0[:, b, :], ALU.mult))
                step(dve.tensor_tensor(t0[:, b, :], rows[:, b, 0, :], lng[:, 1, :], ALU.add))
                step(dve.tensor_tensor(gain[:, 2, b, :], ga, t0[:, b, :], ALU.mult))
                step(dve.tensor_tensor(gain[:, 3, b, :], gb, lng[:, 2, :], ALU.mult))


def mamba_pass(nc, ps, a, bank, ident, sel, cols, mod, gain, norm_c, x_v, yb_v, x1_v, S):
    reverse = ps == 0
    w = "b_" if reverse else "f_"
    FB, BB, DA, HT = bank[0:2], bank[2], bank[3:5], bank[5:7]
    flip = slice(None, None, -1) if reverse else slice(None)
    END = 0 if reverse else T - 1
    fill, drain = (S["fill0"], S["fill1"]), (S["drain0"], S["drain1"])
    SINIT = 3

    with ExitStack() as c:
        def sb(name, shape):
            return c.enter_context(nc.sbuf_tensor(f"{w}{name}", shape, F32))

        w_in = sb("w_in", [P, KM, 2 * DI])
        w_x = sb("w_x", [P, KI, DTR + 2 * DS])
        w_dt = sb("w_dt", [DTR, DI])
        w_out = sb("w_out", [P, KI, DM])
        diag = sb("diag", [P, KI * DCONV, P])
        xin = sb("xin", [P, TS, DM])
        xn = sb("xn", [P, TS, DM])
        stat = sb("stat", [P, TS, 6])
        mv = sb("mv", [P, TS, 4])
        mvk = sb("mvk", [P, BATCH, TS, 4])
        hT = sb("hT", [P, KM, T])
        xpre = sb("xpre", [P, KI, T + HALO])
        halo = sb("halo", [P, BATCH, KI, HALO])
        xi = sb("xi", [P, BATCH, KI, T])
        z = sb("z", [P, BATCH, KI, T])
        dt = sb("dt", [P, BATCH, KI, T])
        u = sb("u", [P, BATCH, KI, T])
        dbB = sb("dbB", [P, BATCH, T])
        Ct = sb("Ct", [P, BATCH, TS, DS])
        Bs = sb("Bs", [P, 2, T])
        dBx = sb("dBx", [P, 4, T])
        h = sb("h", [P, 2, KI, T])
        state = sb("state", [P, BATCH, DS, KI])
        acc = sb("acc", [P, BATCH, TS, DI])
        spt = sb("spt", [P, 2, T])
        ysb = sb("ysb", [P, TS, DM])
        if not reverse:
            ybt = sb("ybt", [P, TS, DM])
            xres = sb("xres", [P, TS, DM])
            dst = sb("dst", [P, TS, 6])
            dmv = sb("dmv", [P, TS, 4])
        block = c.enter_context(nc.Block())
        cv = cols[:, ps, :]

        def job(ch, i):
            if i >= J_LN:
                off = JOBS * ch.d - 12 + i if not ch.first() else i - J_LN
                base = ch.c if not ch.first() else 0
            elif ch.last():
                off, base = PASS_JOBS - TAIL_JOBS + i, 0
            else:
                off, base = JOBS * ch.d + JOBS + 14 + i, ch.c
            return i % 2, base * JOBS + ((off - i % 2) // 2 + PASS_JOBS // 2 * ps)

        def wait_filled(eng, ch, i):
            b, k = job(ch, i)
            eng.wait_ge(fill[b], k + 1)

        def wait_drained(eng, ch, i):
            b, k = job(ch, i)
            eng.wait_ge(drain[b], k + 1)

        def wait_free(eng, ch, i):
            b, k = job(ch, i)
            wait(eng, drain[b], k)

        def schedule(eng, body, flush, prologue):
            prologue(Chunk(ps, 0, 0))
            for d in range(BATCH):
                body(Chunk(ps, 0, d))
            with eng.Fori(1, NC - 1) as c:
                for d in range(BATCH):
                    body(Chunk(ps, c, d))
            for d in range(BATCH):
                body(Chunk(ps, NC - 1, d))
            flush(Chunk(ps, NC - 1, 1))

        @block.sync
        def _(sp):
            for dst, src in ((w_in[:, :, :], a[w + "in_projT"].rearrange("(k p) n -> p k n", p=P)),
                             (w_x[:, :, :], a[w + "x_projT"].rearrange("(k p) n -> p k n", p=P)),
                             (w_dt[:, :], a[w + "dt_wT"]),
                             (w_out[:, :, :], a[w + "out_projT"].rearrange("(k p) n -> p k n", p=P))):
                sp.dma_start(dst, src).then_inc(S["w_in"], 16)

            def load_x(ch):
                wait(sp, S["ln"], ch.at(LNK, -1))
                sp.dma_start(xin[:, :, :], x_v[ch.batch, ch.time(reverse)]).then_inc(S["x_in"], 16)

            def store(ch):
                if reverse:
                    wait_drained(sp, ch, J_OUT + 1)
                    sp.dma_start(yb_v[ch.batch, ch.time(True)], ysb[:, :, :]).then_inc(S["y_out"], 16)
                else:
                    wait(sp, S["comb"], Chunk(0, ch.c, ch.d).at(12, 0))
                    sp.dma_start(ybt[:, :, :], yb_v[ch.batch, ch.time(False)]).then_inc(S["yb_in"], 16)
                    sp.dma_start(xres[:, :, :], x_v[ch.batch, ch.time(False)]).then_inc(S["xr_in"], 16)
                    sp.wait_ge(S["comb"], Chunk(0, ch.c, ch.d).at(12, 12))
                    sp.dma_start(x1_v[ch.batch, ch.time(False)], ysb[:, :, :]).then_inc(S["y_out"], 16)

            def prologue(ch):
                load_x(ch)
                load_x(ch.go(1))

            def body(ch):
                if ch.number() is None or ch.number() + 2 < NCH:
                    load_x(ch.go(2))
                if not ch.first():
                    store(ch.go(-1))

            def flush(ch):
                store(ch)
                sp.wait_ge(S["y_out"], ch.at(16, 16))

            schedule(sp, body, flush, prologue)

        @block.tensor
        def _(pe):
            def front(ch, slot):
                q = ch.batch
                if slot == 4:
                    for k in range(KM):
                        if k == 0:
                            pe.wait_ge(S["ln"], ch.at(LNK, 5))
                        wait_free(pe, ch, J_LN + k)
                        for s in range(TS):
                            mm = pe.transpose(FB[k][:, s * P:(s + 1) * P], xn[:, s, k * P:(k + 1) * P], ident[:, :])
                        mm.then_inc(fill[k], 1)
                if slot in (5, 6, 8):
                    if slot == 5:
                        wait_drained(pe, ch, J_LN + 1)
                    for m in {5: (0, 1), 6: (2, 3), 8: (4, 5, 6, 7)}[slot]:
                        i = J_X + m if m < KI else J_Z + m - KI
                        wait_free(pe, ch, i)
                        for k in range(KM):
                            mm = pe.matmul(FB[i % 2][:, :], w_in[:, k, m * P:(m + 1) * P], hT[:, k, :],
                                           start=(k == 0), stop=(k == KM - 1))
                        mm.then_inc(fill[i % 2], 1)
                if slot == 7:
                    pe.wait_ge(S["halo"], ch.at(2, 1))
                    for m in range(KI):
                        wait_free(pe, ch, J_CONV + m)
                        for k in range(DCONV):
                            o = HALO - k if reverse else k
                            mm = pe.matmul(FB[m % 2][:, :], diag[:, m * DCONV + k, :], xpre[:, m, o:o + T],
                                           start=(k == 0), stop=(k == DCONV - 1))
                        mm.then_inc(fill[m % 2], 1)
                if slot == 9:
                    wait_drained(pe, ch, J_CONV + 3)
                    wait_free(pe, ch, J_B)
                    for k in range(KI):
                        mm = pe.matmul(FB[0][0:B0 + DS, :], w_x[:, k, 0:B0 + DS], xi[:, q, k, :],
                                       start=(k == 0), stop=(k == KI - 1))
                    mm.then_inc(fill[0], 1)
                    wait_free(pe, ch, J_C)
                    for s in range(TS):
                        for k in range(KI):
                            mm = pe.matmul(FB[1][:, s * DS:(s + 1) * DS], xi[:, q, k, s * P:(s + 1) * P],
                                           w_x[:, k, B0 + DS:], start=(k == 0), stop=(k == KI - 1))
                    mm.then_inc(fill[1], 1)
                if slot in (10, 12):
                    for m in ((0, 1) if slot == 10 else (2, 3)):
                        wait_free(pe, ch, J_DT + m)
                        pe.matmul(FB[m % 2][:, :], w_dt[:, m * P:(m + 1) * P], dbB[0:DTR, q, :],
                                  start=True, stop=True).then_inc(fill[m % 2], 1)

            def tail(ch, slot):
                q = ch.batch
                if slot in (1, 2):
                    if slot == 1:
                        pe.wait_ge(S["stt"], ch.at(DS * TS, DS * TS))
                    for m in ((0, 1) if slot == 1 else (2, 3)):
                        wait_free(pe, ch, J_Y + m)
                        for s in range(TS):
                            mm = pe.transpose(FB[m % 2][:, s * P:(s + 1) * P], acc[:, q, s, m * P:(m + 1) * P],
                                              ident[:, :])
                        mm.then_inc(fill[m % 2], 1)
                if slot == 3:
                    pe.wait_ge(S["gate"], ch.at(KI, KI))
                    for i in range(2):
                        wait_free(pe, ch, J_OUT + i)
                        for s in range(2):
                            for k in range(KI):
                                mm = pe.matmul(FB[i][:, s * DM:(s + 1) * DM],
                                               z[:, q, k, (2 * i + s) * P:(2 * i + s + 1) * P], w_out[:, k, :],
                                               start=(k == 0), stop=(k == KI - 1))
                        mm.then_inc(fill[i], 1)

            def spread_b(ch, s):
                if s == 0:
                    wait_drained(pe, ch, J_B)
                wait(pe, S["b_copied"], ch.at(DS, s))
                pe.matmul(BB[:, :], sel[B0:B0 + DS, s, :], dbB[B0:B0 + DS, ch.batch, :],
                          start=True, stop=True).then_inc(S["b_fill"], 1)

            def turn_h(ch, s):
                pe.wait_ge(S["scan"], ch.at(STEPS, KI * (s + 1)))
                for t in range(TS):
                    wait(pe, S["stt"], ch.at(DS * TS, TS * s + t - 1))
                    for m in range(KI):
                        mm = pe.transpose(HT[t % 2][:, m * P:(m + 1) * P], h[:, s % 2, m, t * P:(t + 1) * P],
                                          ident[:, :])
                    mm.then_inc(S["ht_fill"], 1)

            def body(ch):
                for s in range(DS):
                    spread_b(ch, s)
                    if s == 0:
                        if not ch.first():
                            turn_h(ch.go(-1), DS - 1)
                    else:
                        turn_h(ch, s - 1)
                    if not ch.first():
                        tail(ch.go(-1), s)
                    if not ch.last():
                        front(ch.go(1), s)

            def prologue(ch):
                pe.wait_ge(S["w_in"], 64 * (ps + 1))
                pe.wait_ge(S["init"], SINIT * (ps + 1))
                for s in range(DS):
                    front(ch, s)

            def flush(ch):
                turn_h(ch, DS - 1)
                for s in range(DS):
                    tail(ch, s)

            schedule(pe, body, flush, prologue)

        @block.scalar
        def _(act):
            def front(ch, slot):
                q = ch.batch
                if slot == 4:
                    for k in range(KM):
                        wait_filled(act, ch, J_LN + k)
                        act.activation(hT[:, k, :], FB[k][:, :], ACT.Identity, bias=mod[:, k, q:q + 1],
                                       scale=mod[:, 2 + k, q:q + 1]).then_inc(drain[k], 1)
                if slot in (5, 6):
                    lo = 0 if reverse else HALO
                    if slot == 5:
                        wait(act, S["halo"], ch.at(2, -2))
                        act.wait_ge(S["init"], SINIT * (ps + 1))
                        act.copy(xpre[:, :, T:] if reverse else xpre[:, :, 0:HALO],
                                 halo[:, q, :, :]).then_inc(S["halo"], 1)
                    for m in ((0, 1) if slot == 5 else (2, 3)):
                        wait_filled(act, ch, J_X + m)
                        act.copy(xpre[:, m, lo:lo + T], FB[m % 2][:, :]).then_inc(drain[m % 2], 1)
                    if slot == 6:
                        wait_drained(act, ch, J_X + 2)
                        wait_drained(act, ch, J_X + 3)
                        act.wait_ge(S["halo"], ch.at(2, 1))
                        act.copy(halo[:, q, :, :], xpre[:, :, 0:HALO] if reverse else xpre[:, :, T:]
                                 ).then_inc(S["halo"], 1)
                if slot == 7:
                    wait(act, S["gate"], Chunk(ps, ch.c, ch.d - 2).at(KI, KI) if not small(ch) else 0)
                    for m in range(KI):
                        wait_filled(act, ch, J_CONV + m)
                        act.activation(xi[:, q, m, :], FB[m % 2][:, :], ACT.Silu,
                                       bias=cv[:, COL_CB + m:COL_CB + m + 1]).then_inc(drain[m % 2], 1)
                if slot == 8:
                    for m in range(KI):
                        wait_filled(act, ch, J_Z + m)
                        act.activation(z[:, q, m, :], FB[m % 2][:, :], ACT.Silu).then_inc(drain[m % 2], 1)
                if slot == 9:
                    wait_filled(act, ch, J_B)
                    act.copy(dbB[0:B0 + DS, q, :], FB[0][0:B0 + DS, :]).then_inc(drain[0], 1)
                    wait(act, S["stt"], ch.at(DS * TS, -DS * TS) if not small(ch) else 0)
                    wait_filled(act, ch, J_C)
                    act.copy(Ct[:, q, :, :], FB[1][:, 0:TS * DS].rearrange("p (t s) -> p t s", s=DS)
                             ).then_inc(drain[1], 1)
                if slot in (10, 12):
                    for m in ((0, 1) if slot == 10 else (2, 3)):
                        if m >= 2:
                            wait_drained(act, ch, J_DT + m - 2)
                        elif not ch.first():
                            wait_drained(act, ch.go(-1), J_DT + m + 2)
                        wait_filled(act, ch, J_DT + m)
                        act.activation(spt[:, m % 2, :], FB[m % 2][:, :], ACT.Exp,
                                       bias=cv[:, COL_DTB + m:COL_DTB + m + 1]).then_inc(S["exp1"], 1)
                if slot in (11, 13):
                    for m in ((0, 1) if slot == 11 else (2, 3)):
                        act.wait_ge(S["cap"], ch.at(KI, m + 1))
                        act.activation(spt[:, m % 2, :], spt[:, m % 2, :], ACT.Ln, bias=1.0).then_inc(S["lnp"], 1)

            def small(ch):
                return ch.number() is not None and ch.number() < 2

            def tail(ch, slot):
                if slot == 3:
                    if reverse:
                        wait(act, S["y_out"], ch.at(16, 0))
                    else:
                        wait(act, S["y_out"], ch.at(16, 0))
                    for i in range(2):
                        wait_filled(act, ch, J_OUT + i)
                        act.activation(ysb[:, 2 * i:2 * i + 2, :], FB[i][:, :].rearrange("p (s n) -> p s n", s=2),
                                       ACT.Sigmoid).then_inc(drain[i], 1)

            def copy_b(ch, s):
                wait(act, S["dbx"], ch.at(STEPS, KI * (s - 1)))
                act.wait_ge(S["b_fill"], ch.at(DS, s + 1))
                act.copy(Bs[:, s % 2, :], BB[:, :]).then_inc(S["b_copied"], 1)

            def decay(ch, s):
                q = ch.batch
                for m in range(KI):
                    k = KI * s + m
                    if k == 0:
                        wait_drained(act, ch, J_DT + 2)
                        wait_drained(act, ch, J_DT + 3)
                    wait(act, S["scan"], ch.at(STEPS, k - 1))
                    col = COL_A + m * DS + s
                    act.activation(DA[k % 2][:, :], dt[:, q, m, :], ACT.Exp,
                                   scale=cv[:, col:col + 1]).then_inc(S["da"], 1)

            def body(ch):
                for s in range(DS):
                    copy_b(ch, s)
                    decay(ch, s)
                    if not ch.first():
                        tail(ch.go(-1), s)
                    if not ch.last():
                        front(ch.go(1), s)

            def prologue(ch):
                for s in range(DS):
                    front(ch, s)

            def flush(ch):
                for s in range(DS):
                    tail(ch, s)

            schedule(act, body, flush, prologue)

        @block.gpsimd
        def _(pool):
            def front(ch, slot):
                if slot == 2:
                    pool.wait_ge(S["ln"], ch.at(LNK, 2))
                    pool.tensor_tensor(mv[:, :, 3], mv[:, :, 1], norm_c[:, 0, :], ALU.add).then_inc(S["ln"], 1)
                    pool.wait_ge(S["ln"], ch.at(LNK, 3))
                    pool.tensor_tensor(mv[:, :, 2], mv[:, :, 3], norm_c[:, 1, :], ALU.pow).then_inc(S["ln"], 1)

            def tail(ch, slot):
                if slot == 8 and not reverse:
                    f = Chunk(0, ch.c, ch.d)
                    pool.wait_ge(S["comb"], f.at(12, 4))
                    pool.tensor_tensor(dmv[:, :, 3], dmv[:, :, 2], norm_c[:, 1, :], ALU.pow).then_inc(S["comb"], 1)

            def body(ch):
                q = ch.batch
                pool.wait_ge(S["u_ready"], ch.at(KI, KI))
                for s in range(DS):
                    if not ch.first():
                        tail(ch.go(-1), s)
                    if not ch.last():
                        front(ch.go(1), s)
                    pool.wait_ge(S["b_copied"], ch.at(DS, s + 1))
                    for m in range(KI):
                        k = KI * s + m
                        wait(pool, S["scan"], ch.at(STEPS, k - 3))
                        pool.tensor_tensor(dBx[:, k % 4, :], u[:, q, m, :], Bs[:, s % 2, :],
                                           ALU.mult).then_inc(S["dbx"], 1)

            def prologue(ch):
                front(ch, 2)

            def flush(ch):
                tail(ch, 8)

            schedule(pool, body, flush, prologue)

        @block.vector
        def _(dve):
            def front(ch, slot):
                q = ch.batch
                if slot == 0:
                    dve.wait_ge(S["x_in"], ch.at(16, 16))
                    wait(dve, S["ln"], ch.at(LNK, 0))
                    for s in range(TS):
                        ins = dve.bn_stats(stat[:, s, :], xin[:, s, :])
                    ins.then_inc(S["ln"], 1)
                if slot == 1:
                    dve.wait_ge(S["ln"], ch.at(LNK, 1))
                    dve.sem_inc(S["go"], 1)
                    for s in range(TS):
                        ins = dve.bn_aggr(mv[:, s, 0:2], stat[:, s, :])
                    ins.then_inc(S["ln"], 1)
                if slot == 3:
                    dve.wait_ge(S["ln"], ch.at(LNK, 4))
                    if not ch.first():
                        wait_filled(dve, ch.go(-1), J_LN)
                        wait_filled(dve, ch.go(-1), J_LN + 1)
                    for s in range(TS):
                        ins = dve.tensor_scalar(xn[:, s, :], xin[:, s, :], mv[:, s, 0:1], mv[:, s, 2:3],
                                                ALU.subtract, ALU.mult)
                    ins.then_inc(S["ln"], 1)
                if slot in (10, 12):
                    for m in ((0, 1) if slot == 10 else (2, 3)):
                        dve.wait_ge(S["exp1"], ch.at(KI, m + 1))
                        dve.tensor_scalar(spt[:, m % 2, :], spt[:, m % 2, :], EXP_CAP, None,
                                          ALU.min).then_inc(S["cap"], 1)
                if slot in (11, 13):
                    for m in ((0, 1) if slot == 11 else (2, 3)):
                        dve.wait_ge(S["lnp"], ch.at(KI, m + 1))
                        dve.scalar_tensor_tensor(out=dt[:, q, m, :], in0=FB[m % 2][:, :],
                                                 scalar=cv[:, COL_DTB + m:COL_DTB + m + 1], in1=spt[:, m % 2, :],
                                                 op0=ALU.add, op1=ALU.max).then_inc(drain[m % 2], 1)
                if slot == 14:
                    wait_drained(dve, ch, J_DT + 2)
                    wait_drained(dve, ch, J_DT + 3)
                    for m in range(KI):
                        dve.tensor_tensor(u[:, q, m, :], dt[:, q, m, :], xi[:, q, m, :],
                                          ALU.mult).then_inc(S["u_ready"], 1)
                if slot == 15:
                    dve.wait_ge(S["ln"], ch.at(LNK, 5))
                    dve.tensor_copy(mvk[:, q, :, 0:3], mv[:, :, 0:3]).then_inc(S["ln"], 1)

            def tail(ch, slot):
                q = ch.batch
                if slot in (1, 2):
                    for m in ((0, 1) if slot == 1 else (2, 3)):
                        wait_filled(dve, ch, J_Y + m)
                        dve.scalar_tensor_tensor(out=xi[:, q, m, :], in0=xi[:, q, m, :],
                                                 scalar=cv[:, COL_D + m:COL_D + m + 1], in1=FB[m % 2][:, :],
                                                 op0=ALU.mult, op1=ALU.add).then_inc(drain[m % 2], 1)
                    for m in ((0, 1) if slot == 1 else (2, 3)):
                        wait_drained(dve, ch, J_Y + m)
                        if m == 0:
                            wait_drained(dve, ch, J_Z + 3)
                        dve.tensor_tensor(z[:, q, m, :], z[:, q, m, :], xi[:, q, m, :],
                                          ALU.mult).then_inc(S["gate"], 1)
                if not reverse:
                    combine(ch, slot)

            def combine(ch, slot):
                q = ch.batch
                f = Chunk(0, ch.c, ch.d)

                def after(k):
                    wait(dve, S["comb"], f.at(12, k))

                def gains(i):
                    return gain[:, i, q, :].unsqueeze(1).broadcast_to((P, TS, DM))

                if slot == 4:
                    wait_drained(dve, ch, J_OUT)
                    wait_drained(dve, ch, J_OUT + 1)
                    dve.wait_ge(S["yb_in"], f.at(16, 16))
                    dve.tensor_tensor(ysb[:, :, :], ysb[:, :, :], ybt[:, :, :], ALU.add).then_inc(S["comb"], 1)
                if slot == 5:
                    after(1)
                    for s in range(TS):
                        ins = dve.bn_stats(dst[:, s, :], ysb[:, s, :])
                    ins.then_inc(S["comb"], 1)
                if slot == 6:
                    after(2)
                    dve.sem_inc(S["go"], 1)
                    for s in range(TS):
                        ins = dve.bn_aggr(dmv[:, s, 0:2], dst[:, s, :])
                    ins.then_inc(S["comb"], 1)
                if slot == 7:
                    after(3)
                    dve.tensor_scalar(dmv[:, :, 2], dmv[:, :, 1], 0.25, EPS, ALU.mult, ALU.add).then_inc(S["comb"], 1)
                if slot == 9:
                    after(5)
                    for s in range(TS):
                        ins = dve.tensor_scalar(ysb[:, s, :], ysb[:, s, :], dmv[:, s, 0:1], dmv[:, s, 3:4],
                                                ALU.subtract, ALU.mult)
                    ins.then_inc(S["comb"], 1)
                if slot == 10:
                    after(6)
                    dve.tensor_tensor(ysb[:, :, :], ysb[:, :, :], gains(0), ALU.mult).then_inc(S["comb"], 1)
                    dve.wait_ge(S["xr_in"], f.at(16, 16))
                    for s in range(TS):
                        ins = dve.tensor_scalar(ybt[:, s, :], xres[:, s, :], mvk[:, q, s, 0:1], mvk[:, q, s, 2:3],
                                                ALU.subtract, ALU.mult)
                    ins.then_inc(S["comb"], 1)
                if slot == 11:
                    after(8)
                    dve.tensor_tensor(ybt[:, :, :], ybt[:, :, :], gains(1), ALU.mult).then_inc(S["comb"], 1)
                if slot == 12:
                    after(9)
                    dve.tensor_tensor(ysb[:, :, :], ysb[:, :, :], ybt[:, :, :], ALU.add).then_inc(S["comb"], 1)
                if slot == 13:
                    after(10)
                    dve.tensor_tensor(ysb[:, :, :], ysb[:, :, :], xres[:, :, :], ALU.add).then_inc(S["comb"], 1)
                if slot == 14:
                    after(11)
                    dve.tensor_tensor(ysb[:, :, :], ysb[:, :, :], gains(2), ALU.add).then_inc(S["comb"], 1)

            def scan(ch, s, m):
                q = ch.batch
                k = KI * s + m
                if m == 0:
                    wait(dve, S["ht_fill"], ch.at(DS * TS, TS * (s - 1)))
                    wait(dve, S["save"], ch.at(DS, s - 1))
                dve.wait_ge(S["da"], ch.at(STEPS, k + 1))
                dve.wait_ge(S["dbx"], ch.at(STEPS, k + 1))
                dve.tensor_tensor_scan(h[:, s % 2, m, flip], DA[k % 2][:, flip], dBx[:, k % 4, flip],
                                       state[:, q, s, m:m + 1], ALU.mult, ALU.add).then_inc(S["scan"], 1)

            def keep_state(ch, s):
                dve.wait_ge(S["scan"], ch.at(STEPS, KI * (s + 1)))
                dve.tensor_copy(state[:, ch.batch, s, :], h[:, s % 2, :, END]).then_inc(S["save"], 1)

            def weigh(ch, s, t):
                q = ch.batch
                dve.wait_ge(S["ht_fill"], ch.at(DS * TS, TS * s + t + 1))
                scale = Ct[:, q, t, s:s + 1]
                if s == 0:
                    if t == 0:
                        wait_drained(dve, ch, J_C)
                    dve.tensor_scalar(acc[:, q, t, :], HT[t % 2][:, :], scale, None, ALU.mult).then_inc(S["stt"], 1)
                else:
                    dve.wait_ge(S["stt"], ch.at(DS * TS, TS * (s - 1) + t + 1))
                    dve.scalar_tensor_tensor(out=acc[:, q, t, :], in0=HT[t % 2][:, :], scalar=scale,
                                             in1=acc[:, q, t, :], op0=ALU.mult, op1=ALU.add).then_inc(S["stt"], 1)

            def body(ch):
                for s in range(DS):
                    old = (ch, s - 1) if s else (ch.go(-1), DS - 1)
                    for m in range(KI):
                        scan(ch, s, m)
                        if m == 1 and (s or not ch.first()):
                            keep_state(*old)
                        if s or not ch.first():
                            weigh(*old, m)
                    if not ch.first():
                        tail(ch.go(-1), s)
                    if not ch.last():
                        front(ch.go(1), s)

            def prologue(ch):
                dve.wait_ge(S["w_in"], 64 * (ps + 1))
                for k in range(KI * DCONV):
                    ins = dve.tensor_scalar(diag[:, k, :], ident[:, :], cv[:, COL_CW + k:COL_CW + k + 1], None, ALU.mult)
                ins.then_inc(S["init"], 1)
                dve.memset(halo[:, :, :, :], 0.0).then_inc(S["init"], 1)
                dve.memset(state[:, :, :, :], 0.0).then_inc(S["init"], 1)
                dve.wait_ge(S["init"], SINIT * (ps + 1))
                for s in range(DS):
                    front(ch, s)

            def flush(ch):
                keep_state(ch, DS - 1)
                for t in range(TS):
                    weigh(ch, DS - 1, t)
                for s in range(DS):
                    tail(ch, s)

            schedule(dve, body, flush, prologue)


def ffn(nc, sem, sbuf, a, bank, ident, mod, gain, norm_c, fcol, x1_v, out_v):
    F_LN, F_12, F_H1, F_H2, F_3, FJOBS = 0, KM, KM + 2 * KH, KM + 3 * KH, KM + 4 * KH, KM + 4 * KH + 2
    NBK = 4
    FLN = 5
    with ExitStack() as c:
        w1 = sbuf(c, "w1", [P, KM, DH])
        w2 = sbuf(c, "w2", [P, KM, DH])
        h1 = sbuf(c, "h1", [P, KH, DH])
        h2 = sbuf(c, "h2", [P, KH, DH])
        w3 = sbuf(c, "w3", [P, KH, DM])
        x1 = sbuf(c, "x1", [P, BATCH, TS, DM])
        xn = sbuf(c, "xn2", [P, TS, DM])
        stat = sbuf(c, "stat2", [P, TS, 6])
        mv = sbuf(c, "mv2", [P, TS, 4])
        hT = sbuf(c, "hT2", [P, KM, T])
        s1 = sbuf(c, "s1", [P, 2, T])
        ga = sbuf(c, "ga", [P, KH, T])
        gb = sbuf(c, "gb", [P, KH, T])
        ot = sbuf(c, "ot", [P, TS, DM])
        S = {n: c.enter_context(nc.semaphore("f_" + n)) for n in
             ("w_in", "x_in0", "x_in1", "ln", "go", "fin", "o_out", *(f"fill{i}" for i in range(NBK)),
              *(f"drain{i}" for i in range(NBK)))}
        fill = [S[f"fill{i}"] for i in range(NBK)]
        drain = [S[f"drain{i}"] for i in range(NBK)]
        block = c.enter_context(nc.Block())

        def job(ch, i):
            return i % NBK, ch.at(FJOBS // NBK, i // NBK)

        def wait_filled(eng, ch, i):
            b, k = job(ch, i)
            eng.wait_ge(fill[b], k + 1)

        def wait_drained(eng, ch, i):
            b, k = job(ch, i)
            eng.wait_ge(drain[b], k + 1)

        def wait_free(eng, ch, i):
            b, k = job(ch, i)
            wait(eng, drain[b], k)

        def schedule(eng, body):
            for d in range(BATCH):
                body(Chunk(0, 0, d))
            with eng.Fori(1, NC - 1) as c:
                for d in range(BATCH):
                    body(Chunk(0, c, d))
            for d in range(BATCH):
                body(Chunk(0, NC - 1, d))

        @block.sync
        def _(sp):
            def load(ch):
                if ch.number() is None or ch.number() >= BATCH:
                    sp.wait_ge(S["fin"], ch.go(-BATCH).at(2, 2))
                sp.dma_start(x1[:, ch.batch, :, :], x1_v[ch.batch, ch.time(False)]).then_inc(S[f"x_in{ch.batch}"], 16)

            def body(ch):
                if not ch.last():
                    load(ch.go(1))
                sp.wait_ge(S["fin"], ch.at(2, 2))
                sp.sem_inc(S["go"], 1)
                sp.dma_start(out_v[ch.batch, ch.time(False)], ot[:, :, :]).then_inc(S["o_out"], 16)

            load(Chunk(0, 0, 0))
            for dst, name in ((w1, "w1T"), (w2, "w2T"), (h1, "h1T"), (h2, "h2T"), (w3, "w3T")):
                sp.dma_start(dst[:, :, :], a[name].rearrange("(k p) n -> p k n", p=P)).then_inc(S["w_in"], 16)
            schedule(sp, body)
            sp.wait_ge(S["o_out"], 16 * NCH)

        @block.tensor
        def _(pe):
            def layer(ch, i, wt, m, src, kn):
                wait_free(pe, ch, i)
                for k in range(kn):
                    mm = pe.matmul(bank[i % NBK][:, :], wt[:, k, m * P:(m + 1) * P], src[:, k, :],
                                   start=(k == 0), stop=(k == kn - 1))
                mm.then_inc(fill[i % NBK], 1)

            def body(ch):
                for k in range(KM):
                    if k == 0:
                        pe.wait_ge(S["ln"], ch.at(FLN, 5))
                    wait_free(pe, ch, F_LN + k)
                    for s in range(TS):
                        mm = pe.transpose(bank[k][:, s * P:(s + 1) * P], xn[:, s, k * P:(k + 1) * P], ident[:, :])
                    mm.then_inc(fill[k], 1)
                for k in range(KM):
                    wait_drained(pe, ch, F_LN + k)
                for m in range(KH):
                    layer(ch, F_12 + 2 * m, w1, m, hT, KM)
                    layer(ch, F_12 + 2 * m + 1, w2, m, hT, KM)
                for m in (KH - 2, KH - 1):
                    wait_drained(pe, ch, F_12 + 2 * m + 1)
                for m in range(KH):
                    layer(ch, F_H1 + m, h1, m, ga, KH)
                for m in range(KH - NBK, KH):
                    wait_drained(pe, ch, F_H1 + m)
                for m in range(KH):
                    layer(ch, F_H2 + m, h2, m, gb, KH)
                for m in range(KH - NBK, KH):
                    wait_drained(pe, ch, F_H2 + m)
                for i in range(2):
                    b = (F_3 + i) % NBK
                    wait_free(pe, ch, F_3 + i)
                    for s in range(2):
                        for k in range(KH):
                            mm = pe.matmul(bank[b][:, s * DM:(s + 1) * DM], ga[:, k, (2 * i + s) * P:(2 * i + s + 1) * P],
                                           w3[:, k, :], start=(k == 0), stop=(k == KH - 1))
                    mm.then_inc(fill[b], 1)

            pe.wait_ge(S["w_in"], 80)
            schedule(pe, body)

        @block.scalar
        def _(act):
            def body(ch):
                q = ch.batch
                for k in range(KM):
                    wait_filled(act, ch, F_LN + k)
                    act.activation(hT[:, k, :], bank[k][:, :], ACT.Identity, bias=mod[:, 6 + k, q:q + 1],
                                   scale=mod[:, 8 + k, q:q + 1]).then_inc(drain[k], 1)
                for m in range(KH):
                    i = F_12 + 2 * m
                    if m >= 2:
                        wait_drained(act, ch, i - 3)
                    elif not ch.first():
                        wait_drained(act, ch.go(-1), F_12 + 2 * (KH - 2 + m) + 1)
                    wait_filled(act, ch, i)
                    act.activation(s1[:, m % 2, :], bank[i % NBK][:, :], ACT.Silu,
                                   scale=fcol[:, 0, m:m + 1]).then_inc(drain[i % NBK], 1)
                for lay, (base, dst) in enumerate(((F_H1, gb), (F_H2, ga))):
                    for m in range(KH):
                        wait_filled(act, ch, base + m)
                        act.activation(dst[:, m, :], bank[(base + m) % NBK][:, :], ACT.Gelu,
                                       scale=fcol[:, 2 + lay, m:m + 1]).then_inc(drain[(base + m) % NBK], 1)

            schedule(act, body)

        @block.gpsimd
        def _(pool):
            def body(ch):
                pool.wait_ge(S["ln"], ch.at(FLN, 2))
                pool.tensor_tensor(mv[:, :, 3], mv[:, :, 1], norm_c[:, 0, :], ALU.add).then_inc(S["ln"], 1)
                pool.wait_ge(S["ln"], ch.at(FLN, 3))
                pool.tensor_tensor(mv[:, :, 2], mv[:, :, 3], norm_c[:, 1, :], ALU.pow).then_inc(S["ln"], 1)

            schedule(pool, body)

        @block.vector
        def _(dve):
            def norm(ch):
                q = ch.batch
                dve.wait_ge(S[f"x_in{q}"], ch.step * 16 + 16)
                wait(dve, S["ln"], ch.at(FLN, -1))
                for s in range(TS):
                    ins = dve.bn_stats(stat[:, s, :], x1[:, q, s, :])
                ins.then_inc(S["ln"], 1)
                dve.wait_ge(S["ln"], ch.at(FLN, 1))
                dve.sem_inc(S["go"], 1)
                for s in range(TS):
                    ins = dve.bn_aggr(mv[:, s, 0:2], stat[:, s, :])
                ins.then_inc(S["ln"], 1)
                dve.wait_ge(S["ln"], ch.at(FLN, 4))
                if not ch.first():
                    for k in range(KM):
                        wait_filled(dve, ch.go(-1), F_LN + k)
                for s in range(TS):
                    ins = dve.tensor_scalar(xn[:, s, :], x1[:, q, s, :], mv[:, s, 0:1], mv[:, s, 2:3],
                                            ALU.subtract, ALU.mult)
                ins.then_inc(S["ln"], 1)

            def body(ch):
                q = ch.batch
                for m in range(KH):
                    i = F_12 + 2 * m
                    wait_drained(dve, ch, i)
                    wait_filled(dve, ch, i + 1)
                    dve.scalar_tensor_tensor(out=ga[:, m, :], in0=bank[(i + 1) % NBK][:, :], scalar=fcol[:, 1, m:m + 1],
                                             in1=s1[:, m % 2, :], op0=ALU.mult, op1=ALU.mult).then_inc(drain[(i + 1) % NBK], 1)
                if not ch.last():
                    norm(ch.go(1))
                for i in range(2):
                    b = (F_3 + i) % NBK
                    o = ot[:, 2 * i:2 * i + 2, :]
                    wait_filled(dve, ch, F_3 + i)
                    wait(dve, S["o_out"], ch.at(16, 0))
                    dve.tensor_tensor(o, bank[b][:, :].rearrange("p (s n) -> p s n", s=2),
                                      gain[:, 3, q, :].unsqueeze(1).broadcast_to((P, 2, DM)), ALU.mult).then_inc(drain[b], 1)
                    wait_drained(dve, ch, F_3 + i)
                    dve.tensor_tensor(o, o, x1[:, q, 2 * i:2 * i + 2, :], ALU.add).then_inc(S["fin"], 1)

            norm(Chunk(0, 0, 0))
            schedule(dve, body)


def kernel(**inputs):
    import numpy as np
    import concourse.bacc as bacc
    from concourse.bass_utils import run_bass_kernel_spmd

    g = {k: np.asarray(v) for k, v in inputs.items()}
    arrays = {"x": g["L0_attn_x"], "cT": g["L0_c"].T, "wmod": g["L0_wmod"], "ln_g": g["L0_attn_ln_g"],
              "ln_b": g["L0_attn_ln_b"], "w3_s": g["L0_ffn_w3_s"]}

    def by_partition(v):
        return v.reshape(-1, P).T

    for d in "fb":
        m = {n: g[f"L0_attn_{d}_{n}"] for n in ("in_proj", "conv_w", "conv_b", "x_proj", "dt_w", "dt_b", "A_log", "D",
                                                "out_proj")}
        for n in ("in_proj", "x_proj", "dt_w", "out_proj"):
            arrays[f"{d}_{n}T"] = m[n].T
        conv = m["conv_w"].reshape(KI, P, DCONV).transpose(1, 0, 2).reshape(P, -1)
        a_log = m["A_log"].reshape(KI, P, DS).transpose(1, 0, 2).reshape(P, -1)
        arrays[f"{d}_cols"] = np.concatenate([conv, by_partition(m["conv_b"]), by_partition(m["dt_b"]),
                                              by_partition(m["D"]), a_log], axis=1)
    for n in ("w1", "w2", "h1", "h2", "w3"):
        arrays[n + "T"] = g[f"L0_ffn_{n}_w"].T
    arrays["ffn_cols"] = np.stack([by_partition(g[f"L0_ffn_{n}_s"]) for n in ("w1", "w2", "h1", "h2")], axis=1)

    nc = bacc.Bacc("TRN2", target_bir_lowering=False, num_devices=1)
    feeds, aps = {}, {}
    for name, v in arrays.items():
        v = np.ascontiguousarray(v)
        feeds[f"in_{name}"] = v
        aps[name] = nc.dram_tensor(f"in_{name}", v.shape, mybir.dt.from_np(v.dtype), kind="ExternalInput").ap()
    shape = (BATCH, SEQ, DM)
    out = nc.dram_tensor("out", shape, F32, kind="ExternalOutput").ap()
    yb = nc.dram_tensor("yb_dram", shape, F32, kind="Internal").ap()
    x1 = nc.dram_tensor("x1_dram", shape, F32, kind="Internal").ap()
    adaln_mamba_ffn(nc, aps, out, yb, x1)
    r = run_bass_kernel_spmd(nc, [feeds], core_ids=[0])
    return r.results[0]["out"]
```

```python
from contextlib import ExitStack

import concourse.bass as bass
from concourse import mybir

F32 = mybir.dt.float32
ALU = mybir.AluOpType
ACT = mybir.ActivationFunctionType

P = 128
BATCH, SEQ, DM = 2, 4096, 256
DI, DS, DCONV, DTR, DH = 512, 16, 4, 64, 1024
LNK = 5
T = 512
NC = SEQ // T
NCH = BATCH * NC
TS = T // P
KM = DM // P
KI = DI // P
KH = DH // P
HALO = DCONV - 1
B0 = DTR
STEPS = DS * KI
EPS = 1e-5
EXP_CAP = 2.0 ** 60

COL_CW, COL_CB, COL_DTB, COL_D, COL_A = 0, 16, 20, 24, 28
NCOL = COL_A + KI * DS

J_LN, J_Y, J_X, J_CONV, J_B, J_C, J_DT, J_OUT, J_Z = 0, (2, 3, 6, 7), (4, 5, 8, 9), 10, 14, 15, 16, 20, 22
JOBS = 26
TAIL = [*J_Y, J_OUT, J_OUT + 1]
FRONT = [i for i in range(JOBS) if i not in TAIL]
PASS_JOBS = NCH * JOBS
AT_LN, AT_Y, AT_X = 0, (4, 5, 10, 12), (6, 8, 13, 15)
AT_CONV, AT_B, AT_C, AT_DT, AT_OUT, AT_Z = 17, 33, 37, 39, 43, 51
AT_CAP, AT_LNP, AT_MAX = 46, 48, 52
LAG = 2
BP = 4
CBK = 12
SINIT = 3


class Chunk:

    def __init__(self, ps, c, d):
        self.ps, self.c, self.d = ps, c, d
        self.batch = d % BATCH
        self.step = c + d // BATCH if isinstance(c, int) else c + (d // BATCH)

    def go(self, k):
        return Chunk(self.ps, self.c, self.d + k)

    def number(self):
        return BATCH * self.c + self.d if isinstance(self.c, int) else None

    def first(self):
        return self.number() == 0

    def last(self):
        return self.number() == NCH - 1

    def at(self, per_chunk, off):
        return self.c * (BATCH * per_chunk) + (per_chunk * (NCH * self.ps + self.d) + off)

    def time(self, reverse):
        k = self.d // BATCH
        return (self.c * -1) + (NC - 1 - k) if reverse else self.c + k


def wait(eng, sem, value):
    if not (isinstance(value, int) and value <= 0):
        eng.wait_ge(sem, value)


def adaln_mamba_ffn(nc, a, out, yb_dram, x1_dram, b_dram):
    x_v = a["x"].rearrange("b (c s p) d -> b c p s d", s=TS, p=P)
    yb_v = yb_dram.rearrange("b (c s p) d -> b c p s d", s=TS, p=P)
    x1_v = x1_dram.rearrange("b (c s p) d -> b c p s d", s=TS, p=P)
    out_v = out.rearrange("b (c s p) d -> b c p s d", s=TS, p=P)

    with ExitStack() as ctx:
        def sem(name):
            return ctx.enter_context(nc.semaphore(name))

        def sbuf(c, name, shape, dt=F32):
            return c.enter_context(nc.sbuf_tensor(name, shape, dt))

        bank = [ctx.enter_context(nc.psum_tensor(f"bank{i}", [P, T], F32)) for i in range(8)]

        ident = sbuf(ctx, "ident", [P, P])
        cols = sbuf(ctx, "cols", [P, 2, NCOL])
        mod = sbuf(ctx, "mod", [P, 12, BATCH])
        gain = sbuf(ctx, "gain", [P, 4, BATCH, DM])
        norm_c = sbuf(ctx, "norm_c", [P, 2, TS])
        fcol = sbuf(ctx, "fcol", [P, 4, KH])

        setup(nc, ctx, sem, sbuf, a, bank, ident, cols, mod, gain, norm_c, fcol)
        S = {n: sem(n) for n in SEM_NAMES}
        for ps in range(2):
            mamba_pass(nc, ps, a, bank, ident, cols, mod, gain, norm_c, x_v, yb_v, x1_v, b_dram, S)
        ffn(nc, sem, sbuf, a, bank, ident, mod, gain, norm_c, fcol, x1_v, out_v)


SEM_NAMES = [
    "w_in", "init", "go", "x_in", "ln", "fill0", "fill1", "drain0", "drain1", "halo", "sp_exp", "sp_cap", "sp_ln",
    "dt_done", "u_ready", "b_st", "b_in0", "b_in1", "da", "dbx", "scan", "save", "ht_fill", "stt", "gate", "y_out",
    "yb_in", "xr_in", "comb", "kept", "moved",
]


def setup(nc, ctx, sem, sbuf, a, bank, ident, cols, mod, gain, norm_c, fcol):
    with ExitStack() as c:
        ct = sbuf(c, "ct", [P, KM, BATCH])
        cs = sbuf(c, "cs", [P, KM, BATCH])
        cbc = sbuf(c, "cbc", [P, KM, BATCH, P])
        wmod = sbuf(c, "wmod", [P, KM, 6 * DM])
        lng = sbuf(c, "lng", [P, 3, DM])
        rows = sbuf(c, "rows", [P, BATCH, 6, DM])
        ones = sbuf(c, "ones", [P, P])
        sgn = sbuf(c, "sgn", [P, BATCH, DM])
        mag = sbuf(c, "mag", [P, BATCH, DM])
        t0 = sbuf(c, "t0", [P, BATCH, DM])
        s_in, s_pool, s_silu, s_v, s_pe, s_a = (c.enter_context(nc.semaphore(n)) for n in
                                                ("s_in", "s_pool", "s_silu", "s_v", "s_pe", "s_a"))
        block = c.enter_context(nc.Block())

        @block.sync
        def _(sp):
            sp.dma_start(ct[:, :, :], a["cT"].rearrange("(k p) b -> p k b", p=P)).then_inc(s_in, 16)
            sp.dma_start(wmod[:, :, :], a["wmod"].rearrange("(k p) n -> p k n", p=P)).then_inc(s_in, 16)
            sp.dma_start(cols[:, 0, :], a["b_cols"]).then_inc(s_in, 16)
            sp.dma_start(cols[:, 1, :], a["f_cols"]).then_inc(s_in, 16)
            sp.dma_start(fcol[:, :, :], a["ffn_cols"]).then_inc(s_in, 16)
            for i, name in enumerate(("ln_g", "ln_b", "w3_s")):
                sp.dma_start(lng[:, i, :], a[name].partition_broadcast(P)).then_inc(s_in, 16)

        @block.gpsimd
        def _(pool):
            pool.memset(ident[:, :], 0.0).then_inc(s_pool, 1)
            pool.memset(norm_c[:, 0, :], EPS)
            pool.memset(norm_c[:, 1, :], -0.5)
            pool.memset(ones[:, :], 1.0).then_inc(s_pool, 1)
            pool.wait_ge(s_pool, 2)
            pool.affine_select(out=ident[:, :], in_=ident[:, :], compare_op=ALU.not_equal, fill=1.0, base=0,
                               pattern=[[-1, P]], channel_multiplier=1).then_inc(s_pool, 1)

        @block.scalar
        def _(act):
            act.wait_ge(s_in, 128)
            act.activation(cs[:, :, :], ct[:, :, :], ACT.Silu).then_inc(s_silu, 1)
            for d in range(2):
                act.activation(cols[:, d, COL_A:], cols[:, d, COL_A:], ACT.Exp).then_inc(s_a, 1)

        @block.tensor
        def _(pe):
            pe.wait_ge(s_silu, 1)
            for j in range(12):
                for k in range(KM):
                    last = pe.matmul(bank[0][:, 2 * j:2 * j + 2], wmod[:, k, j * P:(j + 1) * P], cs[:, k, :],
                                     start=(k == 0), stop=(k == KM - 1))
            last.then_inc(s_pe, 1)
            pe.wait_ge(s_v, 1)
            for b in range(BATCH):
                for j in range(3):
                    for k in range(KM):
                        last = pe.matmul(bank[1 + 3 * b + j][:, :], cbc[:, k, b, :],
                                         wmod[:, k, 2 * j * DM:2 * (j + 1) * DM], start=(k == 0), stop=(k == KM - 1))
            last.then_inc(s_pe, 1)

        @block.vector
        def _(dve):
            n = [0]

            def step(ins):
                n[0] += 1
                ins.then_inc(s_v, 1)
                dve.wait_ge(s_v, n[0])

            dve.wait_ge(s_silu, 1)
            dve.wait_ge(s_pool, 2)
            for k in range(KM):
                for b in range(BATCH):
                    last = dve.tensor_scalar(cbc[:, k, b, :], ones[:, :], cs[:, k, b:b + 1], None, ALU.mult)
            step(last)
            dve.wait_ge(s_a, 2)
            step(dve.tensor_scalar(cols[:, :, COL_A:], cols[:, :, COL_A:], -1.0, None, ALU.mult))
            dve.wait_ge(s_pe, 1)
            step(dve.tensor_copy(mod[:, :, :], bank[0][:, 0:24].rearrange("p (j b) -> p j b", b=BATCH)))
            for part in (1, 4):
                m = mod[:, 2 * part:2 * part + 2, :]
                step(dve.tensor_scalar(m, m, 1.0, None, ALU.add))
            dve.wait_ge(s_pe, 2)
            for b in range(BATCH):
                for j in range(3):
                    step(dve.tensor_copy(rows[:, b, 2 * j:2 * j + 2, :],
                                         bank[1 + 3 * b + j][:, :].rearrange("p (g n) -> p g n", g=2)))
            for part in (2, 5):
                g = rows[:, :, part, :]
                step(dve.tensor_scalar(sgn[:, :, :], g, 0.0, 2.0, ALU.is_ge, ALU.mult))
                step(dve.tensor_scalar(sgn[:, :, :], sgn[:, :, :], -1.0, None, ALU.add))
                step(dve.tensor_scalar(mag[:, :, :], g, -1.0, 0.25, ALU.mult, ALU.max))
                step(dve.tensor_tensor(mag[:, :, :], mag[:, :, :], g, ALU.max))
                step(dve.tensor_tensor(g, sgn[:, :, :], mag[:, :, :], ALU.mult))
            for b in range(BATCH):
                ga, gb = rows[:, b, 2, :], rows[:, b, 5, :]
                step(dve.scalar_tensor_tensor(out=gain[:, 0, b, :], in0=ga, scalar=0.5, in1=lng[:, 0, :],
                                              op0=ALU.mult, op1=ALU.mult))
                step(dve.tensor_scalar(t0[:, b, :], rows[:, b, 1, :], 1.0, None, ALU.add))
                step(dve.tensor_tensor(gain[:, 1, b, :], ga, t0[:, b, :], ALU.mult))
                step(dve.tensor_tensor(t0[:, b, :], rows[:, b, 0, :], lng[:, 1, :], ALU.add))
                step(dve.tensor_tensor(gain[:, 2, b, :], ga, t0[:, b, :], ALU.mult))
                step(dve.tensor_tensor(gain[:, 3, b, :], gb, lng[:, 2, :], ALU.mult))


def mamba_pass(nc, ps, a, bank, ident, cols, mod, gain, norm_c, x_v, yb_v, x1_v, b_dram, S):
    reverse = ps == 0
    w = "b_" if reverse else "f_"
    FB, DA, HT = bank[0:2], bank[2:6], bank[6:8]
    flip = slice(None, None, -1) if reverse else slice(None)
    END = 0 if reverse else T - 1
    fill, drain = (S["fill0"], S["fill1"]), (S["drain0"], S["drain1"])
    b_in = (S["b_in0"], S["b_in1"])

    with ExitStack() as c:
        def sb(name, shape):
            return c.enter_context(nc.sbuf_tensor(f"{w}{name}", shape, F32))

        w_in = sb("w_in", [P, KM, 2 * DI])
        w_x = sb("w_x", [P, KI, DTR + 2 * DS])
        w_dt = sb("w_dt", [DTR, DI])
        w_out = sb("w_out", [P, KI, DM])
        diag = sb("diag", [P, KI * DCONV, P])
        xin = sb("xin", [P, TS, DM])
        xn = sb("xn", [P, TS, DM])
        stat = sb("stat", [P, TS, 6])
        mv = sb("mv", [P, TS, 4])
        hT = sb("hT", [P, KM, T])
        xpre = sb("xpre", [P, KI, T + HALO])
        halo = sb("halo", [P, BATCH, KI, HALO])
        xi = sb("xi", [P, BATCH, KI, T])
        z = sb("z", [P, BATCH, KI, T])
        dt = sb("dt", [P, BATCH, KI, T])
        u = sb("u", [P, BATCH, KI, T])
        dbB = sb("dbB", [P, T])
        Ct = sb("Ct", [P, BATCH, TS, DS])
        Bs = sb("Bs", [P, 2, BP, T])
        dBx = sb("dBx", [P, 2, KI, T])
        h = sb("h", [P, 2, KI, T])
        state = sb("state", [P, BATCH, DS, KI])
        acc = sb("acc", [P, BATCH, TS, DI])
        ysb = sb("ysb", [P, TS, DM])
        if not reverse:
            ybt = sb("ybt", [P, TS, DM])
            xres = sb("xres", [P, TS, DM])
            dst = sb("dst", [P, TS, 6])
            dmv = sb("dmv", [P, TS, 4])
            mva = sb("mva", [P, BATCH, TS, 4])
            mvb = sb("mvb", [P, BATCH, TS, 4])
        block = c.enter_context(nc.Block())
        cv = cols[:, ps, :]

        def job(ch, i):
            if i in TAIL:
                if ch.last():
                    base, off = 0, PASS_JOBS - len(TAIL) + TAIL.index(i)
                elif ch.number() == NCH - 2:
                    base, off = 0, PASS_JOBS - 2 * len(TAIL) + TAIL.index(i)
                else:
                    base, off = ch.c, JOBS * ch.d + 2 * len(FRONT) + i
            elif ch.first() or ch.number() == 1:
                base, off = 0, len(FRONT) * ch.number() + FRONT.index(i)
            else:
                base, off = ch.c, JOBS * ch.d + 2 * (len(FRONT) - JOBS) + i
            return i % 2, base * JOBS + ((off - i % 2) // 2 + PASS_JOBS // 2 * ps)

        def wait_filled(eng, ch, i):
            b, k = job(ch, i)
            eng.wait_ge(fill[b], k + 1)

        def wait_drained(eng, ch, i):
            b, k = job(ch, i)
            eng.wait_ge(drain[b], k + 1)

        def wait_free(eng, ch, i):
            b, k = job(ch, i)
            wait(eng, drain[b], k)

        def schedule(eng, body, flush, prologue):
            prologue(Chunk(ps, 0, 0))
            for d in range(BATCH):
                body(Chunk(ps, 0, d))
            with eng.Fori(1, NC - 1) as c:
                for d in range(BATCH):
                    body(Chunk(ps, c, d))
            for d in range(BATCH):
                body(Chunk(ps, NC - 1, d))
            flush(Chunk(ps, NC - 1, 1))

        def has(ch, k):
            return ch.number() is None or 0 <= ch.number() + k < NCH

        @block.sync
        def _(sp):
            for dst, src in ((w_in[:, :, :], a[w + "in_projT"].rearrange("(k p) n -> p k n", p=P)),
                             (w_x[:, :, :], a[w + "x_projT"].rearrange("(k p) n -> p k n", p=P)),
                             (w_dt[:, :], a[w + "dt_wT"]),
                             (w_out[:, :, :], a[w + "out_projT"].rearrange("(k p) n -> p k n", p=P))):
                sp.dma_start(dst, src).then_inc(S["w_in"], 16)

            def load_x(ch):
                wait(sp, S["ln"], ch.at(LNK, 0))
                sp.dma_start(xin[:, :, :], x_v[ch.batch, ch.time(reverse)]).then_inc(S["x_in"], 16)

            def store_b(ch):
                wait_drained(sp, ch, J_B)
                sp.dma_start(b_dram[ch.batch], dbB[B0:B0 + DS, :]).then_inc(S["b_st"], 16)

            def load_b(ch, j):
                wait(sp, S["dbx"], ch.at(DS, BP * (j - 1)))
                if j == 0:
                    sp.sem_inc(S["go"], 1)
                    sp.wait_ge(S["b_st"], ch.at(16, 16))
                sp.dma_start(Bs[:, j % 2, :, :], b_dram[ch.batch, BP * j:BP * (j + 1), :].partition_broadcast(P)
                             ).then_inc(b_in[j % 2], 16)

            def load_join(ch):
                f = Chunk(0, ch.c, ch.d)
                wait(sp, S["comb"], f.at(CBK, 0))
                sp.dma_start(ybt[:, :, :], yb_v[ch.batch, ch.time(False)]).then_inc(S["yb_in"], 16)
                sp.dma_start(xres[:, :, :], x_v[ch.batch, ch.time(False)]).then_inc(S["xr_in"], 16)

            def store_x1(ch):
                sp.wait_ge(S["comb"], Chunk(0, ch.c, ch.d).at(CBK, CBK))
                sp.dma_start(x1_v[ch.batch, ch.time(False)], ysb[:, :, :]).then_inc(S["y_out"], 16)

            def store_y(ch):
                wait_drained(sp, ch, J_OUT + 1)
                sp.dma_start(yb_v[ch.batch, ch.time(True)], ysb[:, :, :]).then_inc(S["y_out"], 16)

            def prologue(ch):
                load_x(ch)
                load_x(ch.go(1))
                store_b(ch)
                load_b(ch, 0)
                load_b(ch, 1)

            def body(ch):
                if has(ch, 2):
                    load_x(ch.go(2))
                load_b(ch, 2)
                load_b(ch, 3)
                if not reverse:
                    if has(ch, -2):
                        store_x1(ch.go(-2))
                    if has(ch, -1):
                        load_join(ch.go(-1))
                if has(ch, 1):
                    store_b(ch.go(1))
                    load_b(ch.go(1), 0)
                if reverse and has(ch, -1):
                    store_y(ch.go(-1))
                if has(ch, 1):
                    load_b(ch.go(1), 1)

            def flush(ch):
                if reverse:
                    store_y(ch)
                else:
                    store_x1(ch.go(-1))
                    load_join(ch)
                    store_x1(ch)
                sp.wait_ge(S["y_out"], ch.at(16, 16))

            schedule(sp, body, flush, prologue)

        @block.tensor
        def _(pe):
            def turn(i, src, m, ch):
                wait_free(pe, ch, i)
                for s in range(TS):
                    mm = pe.transpose(FB[i % 2][:, s * P:(s + 1) * P], src(s), ident[:, :])
                mm.then_inc(fill[i % 2], 1)

            def part(ch, i, k, kn, lhsT, rhs, rows=P):
                if k == 0:
                    wait_free(pe, ch, i)
                mm = pe.matmul(FB[i % 2][0:rows, :], lhsT, rhs, start=(k == 0), stop=(k == kn - 1))
                if k == kn - 1:
                    mm.then_inc(fill[i % 2], 1)

            def front(ch, g):
                q = ch.batch
                for k in range(KM):
                    if g == AT_LN + k:
                        if k == 0:
                            pe.wait_ge(S["ln"], ch.at(LNK, LNK))
                        turn(J_LN + k, lambda s: xn[:, s, k * P:(k + 1) * P], k, ch)
                for m in range(KI):
                    k = g - AT_X[m]
                    if 0 <= k < KM:
                        if m == 0 and k == 0:
                            wait_drained(pe, ch, J_LN)
                            wait_drained(pe, ch, J_LN + 1)
                        part(ch, J_X[m], k, KM, w_in[:, k, m * P:(m + 1) * P], hT[:, k, :])
                    k = g - AT_CONV - DCONV * m
                    if 0 <= k < DCONV:
                        if k == 0:
                            if m == 0:
                                pe.wait_ge(S["halo"], ch.at(2, 2))
                        o = HALO - k if reverse else k
                        part(ch, J_CONV + m, k, DCONV, diag[:, m * DCONV + k, :], xpre[:, m, o:o + T])
                    if g == AT_DT + m:
                        part(ch, J_DT + m, 0, 1, w_dt[:, m * P:(m + 1) * P], dbB[0:DTR, :])
                    k = g - AT_Z - KM * m
                    if 0 <= k < KM:
                        part(ch, J_Z + m, k, KM, w_in[:, k, (KI + m) * P:(KI + m + 1) * P], hT[:, k, :])
                    if g == AT_B + m:
                        if m == 0:
                            wait_drained(pe, ch, J_CONV + KI - 1)
                        part(ch, J_B, m, KI, w_x[:, m, 0:B0 + DS], xi[:, q, m, :], B0 + DS)
                for half in range(2):
                    if g == AT_C + half:
                        if half == 0:
                            wait_free(pe, ch, J_C)
                        for s in (2 * half, 2 * half + 1):
                            for k in range(KI):
                                mm = pe.matmul(FB[J_C % 2][:, s * DS:(s + 1) * DS], xi[:, q, k, s * P:(s + 1) * P],
                                               w_x[:, k, B0 + DS:], start=(k == 0), stop=(k == KI - 1))
                        if half == 1:
                            mm.then_inc(fill[J_C % 2], 1)

            def tail(ch, g):
                q = ch.batch
                for m in range(KI):
                    if g == AT_Y[m]:
                        if m == 0:
                            pe.wait_ge(S["stt"], ch.at(STEPS, STEPS))
                        turn(J_Y[m], lambda s: acc[:, q, s, m * P:(m + 1) * P], m, ch)
                for i in range(2):
                    r = g - AT_OUT - 4 * i
                    if 0 <= r < 4:
                        if r == 0:
                            if i == 0:
                                pe.wait_ge(S["gate"], ch.at(1, 1))
                            wait_free(pe, ch, J_OUT + i)
                        s = 2 * i + r // 2
                        for k in (0, 1) if r % 2 == 0 else (2, 3):
                            mm = pe.matmul(FB[i][:, (r // 2) * DM:(r // 2 + 1) * DM], z[:, q, k, s * P:(s + 1) * P],
                                           w_out[:, k, :], start=(k == 0), stop=(k == KI - 1))
                        if r == 3:
                            mm.then_inc(fill[i], 1)

            def turn_h(ch, s, t):
                if t == 0:
                    pe.wait_ge(S["scan"], ch.at(STEPS, KI * (s + 1)))
                wait(pe, S["stt"], ch.at(STEPS, TS * s + t - 1))
                for m in range(KI):
                    mm = pe.transpose(HT[t % 2][:, m * P:(m + 1) * P], h[:, s % 2, m, t * P:(t + 1) * P], ident[:, :])
                mm.then_inc(S["ht_fill"], 1)

            def body(ch):
                for s in range(DS):
                    for t in range(TS):
                        if s:
                            turn_h(ch, s - 1, t)
                        elif has(ch, -1):
                            turn_h(ch.go(-1), DS - 1, t)
                        if has(ch, -1):
                            tail(ch.go(-1), TS * s + t)
                        if has(ch, 1):
                            front(ch.go(1), TS * s + t)

            def prologue(ch):
                pe.wait_ge(S["w_in"], 64 * (ps + 1))
                pe.wait_ge(S["init"], SINIT * (ps + 1))
                for g in range(STEPS):
                    front(ch, g)

            def flush(ch):
                for t in range(TS):
                    turn_h(ch, DS - 1, t)
                for g in range(STEPS):
                    tail(ch, g)

            schedule(pe, body, flush, prologue)

        @block.scalar
        def _(act):
            def front(ch, g):
                q = ch.batch
                for k in range(KM):
                    if g == AT_LN + k + LAG:
                        wait_filled(act, ch, J_LN + k)
                        act.activation(hT[:, k, :], FB[k][:, :], ACT.Identity, bias=mod[:, k, q:q + 1],
                                       scale=mod[:, 2 + k, q:q + 1]).then_inc(drain[k], 1)
                lo = 0 if reverse else HALO
                for m in range(KI):
                    if g == AT_X[m] + KM - 1 + LAG:
                        if m == 0:
                            wait(act, S["halo"], ch.at(2, -2))
                            act.wait_ge(S["init"], SINIT * (ps + 1))
                            act.copy(xpre[:, :, T:] if reverse else xpre[:, :, 0:HALO],
                                     halo[:, q, :, :]).then_inc(S["halo"], 1)
                        wait_filled(act, ch, J_X[m])
                        act.copy(xpre[:, m, lo:lo + T], FB[J_X[m] % 2][:, :]).then_inc(drain[J_X[m] % 2], 1)
                        if m == KI - 1:
                            wait_drained(act, ch, J_X[KI - 2])
                            wait_drained(act, ch, J_X[KI - 1])
                            act.wait_ge(S["halo"], ch.at(2, 1))
                            act.copy(halo[:, q, :, :], xpre[:, :, 0:HALO] if reverse else xpre[:, :, T:]
                                     ).then_inc(S["halo"], 1)
                for m in (0, 2):
                    if g == AT_CONV + DCONV * (m + 2) - 1 + LAG:
                        if m == 0:
                            wait(act, S["gate"], ch.at(1, -1))
                        for i in (m, m + 1):
                            wait_filled(act, ch, J_CONV + i)
                            act.activation(xi[:, q, i, :], FB[i % 2][:, :], ACT.Silu,
                                           bias=cv[:, COL_CB + i:COL_CB + i + 1]).then_inc(drain[i % 2], 1)
                    if g == AT_Z + KM * (m + 2) - 1 + LAG:
                        for i in (m, m + 1):
                            wait_filled(act, ch, J_Z + i)
                            act.activation(z[:, q, i, :], FB[i % 2][:, :], ACT.Silu).then_inc(drain[i % 2], 1)
                if g == AT_B + KI - 1 + LAG:
                    wait(act, S["b_st"], ch.at(16, 0))
                    wait_filled(act, ch, J_B)
                    act.copy(dbB[0:B0 + DS, :], FB[J_B % 2][0:B0 + DS, :]).then_inc(drain[J_B % 2], 1)
                if g == AT_C + 1 + LAG:
                    wait(act, S["stt"], ch.at(STEPS, -STEPS))
                    wait_filled(act, ch, J_C)
                    act.copy(Ct[:, q, :, :], FB[J_C % 2][:, 0:TS * DS].rearrange("p (t s) -> p t s", s=DS)
                             ).then_inc(drain[J_C % 2], 1)
                for m in range(KI):
                    if g == AT_DT + m + LAG:
                        wait_filled(act, ch, J_DT + m)
                        bias = cv[:, COL_DTB + m:COL_DTB + m + 1]
                        act.activation(u[:, q, m, :], FB[m % 2][:, :], ACT.Exp, bias=bias).then_inc(S["sp_exp"], 1)
                        act.activation(dt[:, q, m, :], FB[m % 2][:, :], ACT.Identity, bias=bias).then_inc(drain[m % 2], 1)
                if g == AT_LNP:
                    act.wait_ge(S["sp_cap"], ch.at(1, 1))
                    act.activation(u[:, q, :, :], u[:, q, :, :], ACT.Ln, bias=1.0).then_inc(S["sp_ln"], 1)

            def tail(ch, g):
                if g == AT_OUT + 7 + LAG:
                    wait(act, S["y_out"], ch.at(16, 0))
                    for i in range(2):
                        wait_filled(act, ch, J_OUT + i)
                        act.activation(ysb[:, 2 * i:2 * i + 2, :], FB[i][:, :].rearrange("p (s n) -> p s n", s=2),
                                       ACT.Sigmoid).then_inc(drain[i], 1)

            def decay(ch, k):
                s, m = divmod(k, KI)
                if k == 0:
                    act.wait_ge(S["dt_done"], ch.at(1, 1))
                wait(act, S["scan"], ch.at(STEPS, k - 3))
                col = COL_A + m * DS + s
                act.activation(DA[k % 4][:, :], dt[:, ch.batch, m, :], ACT.Exp, scale=cv[:, col:col + 1]
                               ).then_inc(S["da"], 1)

            def body(ch):
                for k in range(STEPS):
                    decay(ch, k)
                    if has(ch, -1):
                        tail(ch.go(-1), k)
                    if has(ch, 1):
                        front(ch.go(1), k)

            def prologue(ch):
                for g in range(STEPS):
                    front(ch, g)

            def flush(ch):
                for g in range(STEPS):
                    tail(ch, g)

            schedule(act, body, flush, prologue)

        @block.gpsimd
        def _(pool):
            def norm(ch):
                pool.wait_ge(S["ln"], ch.at(LNK, 2))
                pool.tensor_tensor(mv[:, :, 2], mv[:, :, 1], norm_c[:, 0, :], ALU.add).then_inc(S["ln"], 1)
                pool.wait_ge(S["ln"], ch.at(LNK, 3))
                pool.tensor_tensor(mv[:, :, 3], mv[:, :, 2], norm_c[:, 1, :], ALU.pow).then_inc(S["ln"], 1)

            def make_u(ch):
                q = ch.batch
                pool.wait_ge(S["dt_done"], ch.at(1, 1))
                pool.tensor_tensor(u[:, q, :, :], dt[:, q, :, :], xi[:, q, :, :], ALU.mult).then_inc(S["u_ready"], 1)

            def gate(ch):
                q = ch.batch
                wait_drained(pool, ch, J_Y[2])
                wait_drained(pool, ch, J_Y[3])
                pool.tensor_tensor(z[:, q, :, :], z[:, q, :, :], xi[:, q, :, :], ALU.mult).then_inc(S["gate"], 1)

            def join(ch):
                f = Chunk(0, ch.c, ch.d)
                pool.wait_ge(S["comb"], f.at(CBK, 4))
                pool.tensor_tensor(dmv[:, :, 3], dmv[:, :, 2], norm_c[:, 1, :], ALU.pow).then_inc(S["comb"], 1)

            def body(ch):
                q = ch.batch
                for s in range(DS):
                    if s == 0:
                        pool.wait_ge(S["u_ready"], ch.at(1, 1))
                    if s % BP == 0:
                        j = s // BP
                        pool.wait_ge(b_in[j % 2], ch.at(32, 16 * (j // 2) + 16))
                    wait(pool, S["scan"], ch.at(STEPS, KI * (s - 1)))
                    pool.tensor_tensor(dBx[:, s % 2, :, :], u[:, q, :, :],
                                       Bs[:, (s // BP) % 2, s % BP, :].unsqueeze(1).broadcast_to((P, KI, T)),
                                       ALU.mult).then_inc(S["dbx"], 1)
                    if s == 4 and not reverse and has(ch, -2):
                        join(ch.go(-2))
                    if s == 6 and has(ch, -1):
                        gate(ch.go(-1))
                    if s == DS - 1 and has(ch, 1):
                        make_u(ch.go(1))
                    if s == DS - 1 and has(ch, 2):
                        norm(ch.go(2))

            def prologue(ch):
                norm(ch)
                make_u(ch)
                norm(ch.go(1))

            def flush(ch):
                if not reverse:
                    join(ch.go(-1))
                gate(ch)
                if not reverse:
                    join(ch)

            schedule(pool, body, flush, prologue)

        @block.vector
        def _(dve):
            def norm(ch, slot):
                if slot == 11:
                    dve.wait_ge(S["x_in"], ch.at(16, 16))
                    wait(dve, S["ln"], ch.at(LNK, 0))
                    for s in range(TS):
                        ins = dve.bn_stats(stat[:, s, :], xin[:, s, :])
                    ins.then_inc(S["ln"], 1)
                if slot == 12:
                    if not reverse:
                        wait(dve, S["kept"], Chunk(0, ch.c, ch.d).at(1, 0))
                        dve.sem_inc(S["go"], 1)
                    dve.wait_ge(S["ln"], ch.at(LNK, 1))
                    dve.sem_inc(S["go"], 1)
                    for s in range(TS):
                        ins = dve.bn_aggr(mv[:, s, 0:2], stat[:, s, :])
                    ins.then_inc(S["ln"], 1)
                if slot == 15:
                    if not ch.first():
                        wait_filled(dve, ch.go(-1), J_LN)
                        wait_filled(dve, ch.go(-1), J_LN + 1)
                    dve.wait_ge(S["ln"], ch.at(LNK, 4))
                    for s in range(TS):
                        ins = dve.tensor_scalar(xn[:, s, :], xin[:, s, :], mv[:, s, 0:1], mv[:, s, 3:4],
                                                ALU.subtract, ALU.mult)
                    ins.then_inc(S["ln"], 1)

            def keep_moments(ch):
                f = Chunk(0, ch.c, ch.d)
                if has(ch, -1):
                    q = ch.go(-1).batch
                    dve.wait_ge(S["kept"], f.at(1, 0))
                    dve.tensor_copy(mvb[:, q, :, :], mva[:, q, :, :]).then_inc(S["moved"], 1)
                if has(ch, 1):
                    dve.wait_ge(S["ln"], ch.go(1).at(LNK, 4))
                    wait(dve, S["moved"], f.at(1, 0))
                    dve.tensor_copy(mva[:, ch.go(1).batch, :, :], mv[:, :, :]).then_inc(S["kept"], 1)

            def front(ch, g):
                q = ch.batch
                if g == AT_CAP:
                    dve.wait_ge(S["sp_exp"], ch.at(KI, KI))
                    dve.tensor_scalar(u[:, q, :, :], u[:, q, :, :], EXP_CAP, None, ALU.min).then_inc(S["sp_cap"], 1)
                if g == AT_MAX:
                    wait_drained(dve, ch, J_DT + KI - 2)
                    wait_drained(dve, ch, J_DT + KI - 1)
                    dve.wait_ge(S["sp_ln"], ch.at(1, 1))
                    dve.tensor_tensor(dt[:, q, :, :], dt[:, q, :, :], u[:, q, :, :], ALU.max).then_inc(S["dt_done"], 1)

            def tail(ch, g):
                q = ch.batch
                for m in range(KI):
                    if g == AT_Y[m] + LAG:
                        wait_filled(dve, ch, J_Y[m])
                        dve.scalar_tensor_tensor(out=xi[:, q, m, :], in0=xi[:, q, m, :],
                                                 scalar=cv[:, COL_D + m:COL_D + m + 1], in1=FB[J_Y[m] % 2][:, :],
                                                 op0=ALU.mult, op1=ALU.add).then_inc(drain[J_Y[m] % 2], 1)

            def join(ch, slot):
                q = ch.batch
                f = Chunk(0, ch.c, ch.d)

                def after(k):
                    dve.wait_ge(S["comb"], f.at(CBK, k))

                def gains(i):
                    return gain[:, i, q, :].unsqueeze(1).broadcast_to((P, TS, DM))

                if slot == 0:
                    wait_drained(dve, ch, J_OUT)
                    wait_drained(dve, ch, J_OUT + 1)
                    dve.wait_ge(S["yb_in"], f.at(16, 16))
                    dve.tensor_tensor(ysb[:, :, :], ysb[:, :, :], ybt[:, :, :], ALU.add).then_inc(S["comb"], 1)
                if slot == 1:
                    after(1)
                    for s in range(TS):
                        ins = dve.bn_stats(dst[:, s, :], ysb[:, s, :])
                    ins.then_inc(S["comb"], 1)
                if slot == 2:
                    after(2)
                    dve.sem_inc(S["go"], 1)
                    for s in range(TS):
                        ins = dve.bn_aggr(dmv[:, s, 0:2], dst[:, s, :])
                    ins.then_inc(S["comb"], 1)
                if slot == 3:
                    after(3)
                    dve.tensor_scalar(dmv[:, :, 2], dmv[:, :, 1], 0.25, EPS, ALU.mult, ALU.add).then_inc(S["comb"], 1)
                if slot == 5:
                    after(5)
                    for s in range(TS):
                        ins = dve.tensor_scalar(ysb[:, s, :], ysb[:, s, :], dmv[:, s, 0:1], dmv[:, s, 3:4],
                                                ALU.subtract, ALU.mult)
                    ins.then_inc(S["comb"], 1)
                if slot == 6:
                    after(6)
                    dve.tensor_tensor(ysb[:, :, :], ysb[:, :, :], gains(0), ALU.mult).then_inc(S["comb"], 1)
                    dve.wait_ge(S["xr_in"], f.at(16, 16))
                    if has(ch, 1):
                        dve.wait_ge(S["moved"], f.at(1, 1))
                    for s in range(TS):
                        ins = dve.tensor_scalar(ybt[:, s, :], xres[:, s, :], mvb[:, q, s, 0:1], mvb[:, q, s, 3:4],
                                                ALU.subtract, ALU.mult)
                    ins.then_inc(S["comb"], 1)
                if slot == 7:
                    after(8)
                    dve.tensor_tensor(ybt[:, :, :], ybt[:, :, :], gains(1), ALU.mult).then_inc(S["comb"], 1)
                if slot == 8:
                    after(9)
                    dve.tensor_tensor(ysb[:, :, :], ysb[:, :, :], ybt[:, :, :], ALU.add).then_inc(S["comb"], 1)
                if slot == 9:
                    after(10)
                    dve.tensor_tensor(ysb[:, :, :], ysb[:, :, :], xres[:, :, :], ALU.add).then_inc(S["comb"], 1)
                if slot == 10:
                    after(11)
                    dve.tensor_tensor(ysb[:, :, :], ysb[:, :, :], gains(2), ALU.add).then_inc(S["comb"], 1)

            def scan(ch, s, m):
                q = ch.batch
                k = KI * s + m
                if m == 0:
                    wait(dve, S["ht_fill"], ch.at(STEPS, TS * (s - 1)))
                    wait(dve, S["save"], ch.at(DS, s - 1))
                    dve.wait_ge(S["dbx"], ch.at(DS, s + 1))
                dve.wait_ge(S["da"], ch.at(STEPS, k + 1))
                dve.tensor_tensor_scan(h[:, s % 2, m, flip], DA[k % 4][:, flip], dBx[:, s % 2, m, flip],
                                       state[:, q, s, m:m + 1], ALU.mult, ALU.add).then_inc(S["scan"], 1)

            def keep_state(ch, s):
                dve.wait_ge(S["scan"], ch.at(STEPS, KI * (s + 1)))
                dve.tensor_copy(state[:, ch.batch, s, :], h[:, s % 2, :, END]).then_inc(S["save"], 1)

            def weigh(ch, s, t):
                q = ch.batch
                dve.wait_ge(S["ht_fill"], ch.at(STEPS, TS * s + t + 1))
                scale = Ct[:, q, t, s:s + 1]
                if s == 0:
                    if t == 0:
                        wait_drained(dve, ch, J_C)
                    dve.tensor_scalar(acc[:, q, t, :], HT[t % 2][:, :], scale, None, ALU.mult).then_inc(S["stt"], 1)
                else:
                    dve.wait_ge(S["stt"], ch.at(STEPS, TS * (s - 1) + t + 1))
                    dve.scalar_tensor_tensor(out=acc[:, q, t, :], in0=HT[t % 2][:, :], scalar=scale,
                                             in1=acc[:, q, t, :], op0=ALU.mult, op1=ALU.add).then_inc(S["stt"], 1)

            def body(ch):
                for s in range(DS):
                    old = (ch, s - 1) if s else (ch.go(-1), DS - 1)
                    for m in range(KI):
                        scan(ch, s, m)
                        if m == 1 and (s or has(ch, -1)):
                            keep_state(*old)
                        if s or has(ch, -1):
                            weigh(*old, m)
                        if has(ch, -1):
                            tail(ch.go(-1), KI * s + m)
                        if has(ch, 1):
                            front(ch.go(1), KI * s + m)
                    if not reverse and has(ch, -2):
                        join(ch.go(-2), s)
                    if not reverse and s == 9:
                        keep_moments(ch)
                    if has(ch, 2):
                        norm(ch.go(2), s)

            def prologue(ch):
                dve.wait_ge(S["w_in"], 64 * (ps + 1))
                for k in range(KI * DCONV):
                    ins = dve.tensor_scalar(diag[:, k, :], ident[:, :], cv[:, COL_CW + k:COL_CW + k + 1], None, ALU.mult)
                ins.then_inc(S["init"], 1)
                dve.memset(halo[:, :, :, :], 0.0).then_inc(S["init"], 1)
                dve.memset(state[:, :, :, :], 0.0).then_inc(S["init"], 1)
                dve.wait_ge(S["init"], SINIT * (ps + 1))
                for s in range(DS):
                    norm(ch, s)
                if not reverse:
                    dve.tensor_copy(mva[:, 0, :, :], mv[:, :, :]).then_inc(S["kept"], 1)
                for g in range(STEPS):
                    front(ch, g)
                for s in range(DS):
                    norm(ch.go(1), s)

            def flush(ch):
                keep_state(ch, DS - 1)
                for t in range(TS):
                    weigh(ch, DS - 1, t)
                for g in range(STEPS):
                    tail(ch, g)
                if not reverse:
                    for s in range(DS):
                        join(ch.go(-1), s)
                    f = Chunk(0, ch.c, ch.d)
                    dve.wait_ge(S["kept"], f.at(1, 1))
                    dve.tensor_copy(mvb[:, ch.batch, :, :], mva[:, ch.batch, :, :]).then_inc(S["moved"], 1)
                    dve.wait_ge(S["moved"], f.at(1, 1))
                    for s in range(DS):
                        join(ch, s)

            schedule(dve, body, flush, prologue)


def ffn(nc, sem, sbuf, a, bank, ident, mod, gain, norm_c, fcol, x1_v, out_v):
    F_LN, F_12, F_H1, F_H2, F_3, FJOBS = 0, KM, KM + 2 * KH, KM + 3 * KH, KM + 4 * KH, KM + 4 * KH + 2
    NBK = 4
    FLN = 5
    with ExitStack() as c:
        w1 = sbuf(c, "w1", [P, KM, DH])
        w2 = sbuf(c, "w2", [P, KM, DH])
        h1 = sbuf(c, "h1", [P, KH, DH])
        h2 = sbuf(c, "h2", [P, KH, DH])
        w3 = sbuf(c, "w3", [P, KH, DM])
        x1 = sbuf(c, "x1", [P, BATCH, TS, DM])
        xn = sbuf(c, "xn2", [P, TS, DM])
        stat = sbuf(c, "stat2", [P, TS, 6])
        mv = sbuf(c, "mv2", [P, TS, 4])
        hT = sbuf(c, "hT2", [P, KM, T])
        s1 = sbuf(c, "s1", [P, 2, T])
        ga = sbuf(c, "ga", [P, KH, T])
        gb = sbuf(c, "gb", [P, KH, T])
        ot = sbuf(c, "ot", [P, TS, DM])
        S = {n: c.enter_context(nc.semaphore("f_" + n)) for n in
             ("w_in", "x_in0", "x_in1", "ln", "go", "fin", "o_out", *(f"fill{i}" for i in range(NBK)),
              *(f"drain{i}" for i in range(NBK)))}
        fill = [S[f"fill{i}"] for i in range(NBK)]
        drain = [S[f"drain{i}"] for i in range(NBK)]
        block = c.enter_context(nc.Block())

        def job(ch, i):
            return i % NBK, ch.at(FJOBS // NBK, i // NBK)

        def wait_filled(eng, ch, i):
            b, k = job(ch, i)
            eng.wait_ge(fill[b], k + 1)

        def wait_drained(eng, ch, i):
            b, k = job(ch, i)
            eng.wait_ge(drain[b], k + 1)

        def wait_free(eng, ch, i):
            b, k = job(ch, i)
            wait(eng, drain[b], k)

        def schedule(eng, body):
            for d in range(BATCH):
                body(Chunk(0, 0, d))
            with eng.Fori(1, NC - 1) as c:
                for d in range(BATCH):
                    body(Chunk(0, c, d))
            for d in range(BATCH):
                body(Chunk(0, NC - 1, d))

        @block.sync
        def _(sp):
            def load(ch):
                if ch.number() is None or ch.number() >= BATCH:
                    sp.wait_ge(S["fin"], ch.go(-BATCH).at(2, 2))
                sp.dma_start(x1[:, ch.batch, :, :], x1_v[ch.batch, ch.time(False)]).then_inc(S[f"x_in{ch.batch}"], 16)

            def body(ch):
                if not ch.last():
                    load(ch.go(1))
                sp.wait_ge(S["fin"], ch.at(2, 2))
                sp.sem_inc(S["go"], 1)
                sp.dma_start(out_v[ch.batch, ch.time(False)], ot[:, :, :]).then_inc(S["o_out"], 16)

            load(Chunk(0, 0, 0))
            for dst, name in ((w1, "w1T"), (w2, "w2T"), (h1, "h1T"), (h2, "h2T"), (w3, "w3T")):
                sp.dma_start(dst[:, :, :], a[name].rearrange("(k p) n -> p k n", p=P)).then_inc(S["w_in"], 16)
            schedule(sp, body)
            sp.wait_ge(S["o_out"], 16 * NCH)

        @block.tensor
        def _(pe):
            def layer(ch, i, wt, m, src, kn):
                wait_free(pe, ch, i)
                for k in range(kn):
                    mm = pe.matmul(bank[i % NBK][:, :], wt[:, k, m * P:(m + 1) * P], src[:, k, :],
                                   start=(k == 0), stop=(k == kn - 1))
                mm.then_inc(fill[i % NBK], 1)

            def body(ch):
                for k in range(KM):
                    if k == 0:
                        pe.wait_ge(S["ln"], ch.at(FLN, 5))
                    wait_free(pe, ch, F_LN + k)
                    for s in range(TS):
                        mm = pe.transpose(bank[k][:, s * P:(s + 1) * P], xn[:, s, k * P:(k + 1) * P], ident[:, :])
                    mm.then_inc(fill[k], 1)
                for k in range(KM):
                    wait_drained(pe, ch, F_LN + k)
                for m in range(KH):
                    layer(ch, F_12 + 2 * m, w1, m, hT, KM)
                    layer(ch, F_12 + 2 * m + 1, w2, m, hT, KM)
                for m in (KH - 2, KH - 1):
                    wait_drained(pe, ch, F_12 + 2 * m + 1)
                for m in range(KH):
                    layer(ch, F_H1 + m, h1, m, ga, KH)
                for m in range(KH - NBK, KH):
                    wait_drained(pe, ch, F_H1 + m)
                for m in range(KH):
                    layer(ch, F_H2 + m, h2, m, gb, KH)
                for m in range(KH - NBK, KH):
                    wait_drained(pe, ch, F_H2 + m)
                for i in range(2):
                    b = (F_3 + i) % NBK
                    wait_free(pe, ch, F_3 + i)
                    for s in range(2):
                        for k in range(KH):
                            mm = pe.matmul(bank[b][:, s * DM:(s + 1) * DM], ga[:, k, (2 * i + s) * P:(2 * i + s + 1) * P],
                                           w3[:, k, :], start=(k == 0), stop=(k == KH - 1))
                    mm.then_inc(fill[b], 1)

            pe.wait_ge(S["w_in"], 80)
            schedule(pe, body)

        @block.scalar
        def _(act):
            def body(ch):
                q = ch.batch
                for k in range(KM):
                    wait_filled(act, ch, F_LN + k)
                    act.activation(hT[:, k, :], bank[k][:, :], ACT.Identity, bias=mod[:, 6 + k, q:q + 1],
                                   scale=mod[:, 8 + k, q:q + 1]).then_inc(drain[k], 1)
                for m in range(KH):
                    i = F_12 + 2 * m
                    if m >= 2:
                        wait_drained(act, ch, i - 3)
                    elif not ch.first():
                        wait_drained(act, ch.go(-1), F_12 + 2 * (KH - 2 + m) + 1)
                    wait_filled(act, ch, i)
                    act.activation(s1[:, m % 2, :], bank[i % NBK][:, :], ACT.Silu,
                                   scale=fcol[:, 0, m:m + 1]).then_inc(drain[i % NBK], 1)
                for lay, (base, dst) in enumerate(((F_H1, gb), (F_H2, ga))):
                    for m in range(KH):
                        wait_filled(act, ch, base + m)
                        act.activation(dst[:, m, :], bank[(base + m) % NBK][:, :], ACT.Gelu,
                                       scale=fcol[:, 2 + lay, m:m + 1]).then_inc(drain[(base + m) % NBK], 1)

            schedule(act, body)

        @block.gpsimd
        def _(pool):
            def body(ch):
                pool.wait_ge(S["ln"], ch.at(FLN, 2))
                pool.tensor_tensor(mv[:, :, 3], mv[:, :, 1], norm_c[:, 0, :], ALU.add).then_inc(S["ln"], 1)
                pool.wait_ge(S["ln"], ch.at(FLN, 3))
                pool.tensor_tensor(mv[:, :, 2], mv[:, :, 3], norm_c[:, 1, :], ALU.pow).then_inc(S["ln"], 1)

            schedule(pool, body)

        @block.vector
        def _(dve):
            def norm(ch):
                q = ch.batch
                dve.wait_ge(S[f"x_in{q}"], ch.step * 16 + 16)
                wait(dve, S["ln"], ch.at(FLN, -1))
                for s in range(TS):
                    ins = dve.bn_stats(stat[:, s, :], x1[:, q, s, :])
                ins.then_inc(S["ln"], 1)
                dve.wait_ge(S["ln"], ch.at(FLN, 1))
                dve.sem_inc(S["go"], 1)
                for s in range(TS):
                    ins = dve.bn_aggr(mv[:, s, 0:2], stat[:, s, :])
                ins.then_inc(S["ln"], 1)
                dve.wait_ge(S["ln"], ch.at(FLN, 4))
                if not ch.first():
                    for k in range(KM):
                        wait_filled(dve, ch.go(-1), F_LN + k)
                for s in range(TS):
                    ins = dve.tensor_scalar(xn[:, s, :], x1[:, q, s, :], mv[:, s, 0:1], mv[:, s, 2:3],
                                            ALU.subtract, ALU.mult)
                ins.then_inc(S["ln"], 1)

            def body(ch):
                q = ch.batch
                for m in range(KH):
                    i = F_12 + 2 * m
                    wait_drained(dve, ch, i)
                    wait_filled(dve, ch, i + 1)
                    dve.scalar_tensor_tensor(out=ga[:, m, :], in0=bank[(i + 1) % NBK][:, :], scalar=fcol[:, 1, m:m + 1],
                                             in1=s1[:, m % 2, :], op0=ALU.mult, op1=ALU.mult).then_inc(drain[(i + 1) % NBK], 1)
                if not ch.last():
                    norm(ch.go(1))
                for i in range(2):
                    b = (F_3 + i) % NBK
                    o = ot[:, 2 * i:2 * i + 2, :]
                    wait_filled(dve, ch, F_3 + i)
                    wait(dve, S["o_out"], ch.at(16, 0))
                    dve.tensor_tensor(o, bank[b][:, :].rearrange("p (s n) -> p s n", s=2),
                                      gain[:, 3, q, :].unsqueeze(1).broadcast_to((P, 2, DM)), ALU.mult).then_inc(drain[b], 1)
                    wait_drained(dve, ch, F_3 + i)
                    dve.tensor_tensor(o, o, x1[:, q, 2 * i:2 * i + 2, :], ALU.add).then_inc(S["fin"], 1)

            norm(Chunk(0, 0, 0))
            schedule(dve, body)


def kernel(**inputs):
    import numpy as np
    import concourse.bacc as bacc
    from concourse.bass_utils import run_bass_kernel_spmd

    g = {k: np.asarray(v) for k, v in inputs.items()}
    arrays = {"x": g["L0_attn_x"], "cT": g["L0_c"].T, "wmod": g["L0_wmod"], "ln_g": g["L0_attn_ln_g"],
              "ln_b": g["L0_attn_ln_b"], "w3_s": g["L0_ffn_w3_s"]}

    def by_partition(v):
        return v.reshape(-1, P).T

    for d in "fb":
        m = {n: g[f"L0_attn_{d}_{n}"] for n in ("in_proj", "conv_w", "conv_b", "x_proj", "dt_w", "dt_b", "A_log", "D",
                                                "out_proj")}
        for n in ("in_proj", "x_proj", "dt_w", "out_proj"):
            arrays[f"{d}_{n}T"] = m[n].T
        conv = m["conv_w"].reshape(KI, P, DCONV).transpose(1, 0, 2).reshape(P, -1)
        a_log = m["A_log"].reshape(KI, P, DS).transpose(1, 0, 2).reshape(P, -1)
        arrays[f"{d}_cols"] = np.concatenate([conv, by_partition(m["conv_b"]), by_partition(m["dt_b"]),
                                              by_partition(m["D"]), a_log], axis=1)
    for n in ("w1", "w2", "h1", "h2", "w3"):
        arrays[n + "T"] = g[f"L0_ffn_{n}_w"].T
    arrays["ffn_cols"] = np.stack([by_partition(g[f"L0_ffn_{n}_s"]) for n in ("w1", "w2", "h1", "h2")], axis=1)

    nc = bacc.Bacc("TRN2", target_bir_lowering=False, num_devices=1)
    feeds, aps = {}, {}
    for name, v in arrays.items():
        v = np.ascontiguousarray(v)
        feeds[f"in_{name}"] = v
        aps[name] = nc.dram_tensor(f"in_{name}", v.shape, mybir.dt.from_np(v.dtype), kind="ExternalInput").ap()
    shape = (BATCH, SEQ, DM)
    out = nc.dram_tensor("out", shape, F32, kind="ExternalOutput").ap()
    yb = nc.dram_tensor("yb_dram", shape, F32, kind="Internal").ap()
    x1 = nc.dram_tensor("x1_dram", shape, F32, kind="Internal").ap()
    b = nc.dram_tensor("b_dram", (BATCH, DS, T), F32, kind="Internal").ap()
    adaln_mamba_ffn(nc, aps, out, yb, x1, b)
    r = run_bass_kernel_spmd(nc, [feeds], core_ids=[0])
    return r.results[0]["out"]
```

```python
from contextlib import ExitStack

import concourse.bass as bass
from concourse import mybir

F32 = mybir.dt.float32
F32R = mybir.dt.float32r
I32 = mybir.dt.int32
ALU = mybir.AluOpType
ACT = mybir.ActivationFunctionType

P = 128
BATCH, SEQ, DM = 2, 4096, 256
DI, DS, DCONV, DTR, DH = 512, 16, 4, 64, 1024
LNK = 5
T = 512
NC = SEQ // T
NCH = BATCH * NC
TS = T // P
KM = DM // P
KI = DI // P
KH = DH // P
HALO = DCONV - 1
B0 = DTR
STEPS = DS * KI
EPS = 1e-5

COL_CW, COL_CB, COL_DTB, COL_D, COL_A = 0, 16, 20, 24, 28
NCOL = COL_A + KI * DS

J_LN, J_X, J_Y, J_CONV = (0, 1), (2, 3, 5, 6), (4, 7, 8, 10), (9, 11, 12, 13)
AT_LN, AT_X, AT_Y, AT_CONV = (0, 1), (5, 7, 10, 15), (9, 14, 15, 18), (17, 21, 25, 29)
J_OUT, J_B, J_C, J_DT, J_Z = (14, 21), 15, 16, (17, 18, 19, 20), (22, 23, 24, 25)
AT_OUT, AT_B, AT_C, AT_DT, AT_Z = (33, 49), 38, 41, (46, 47, 48, 50), (55, 57, 59, 61)
NFB = 3
BANK = (0, 1, 2, 0, 1, 2, 0, 1, 2, 0, 1, 1, 2, 0, 1, 2, 0, 1, 2, 0, 1, 2, 0, 1, 2, 0)
TAIL = [*J_Y, *J_OUT]
FRONT = [i for i in range(len(BANK)) if i not in TAIL]
NDA = 3
SLOT = [k % NDA for k in range(STEPS - 1)] + [1]
ACT_LAG, DVE_LAG = 3, 2
NORM_S = (6, 7, 9)
GATE_S = 6
AT_SILU = (28, 32, 36, 40)
AT_EXP = (54, 57)
AT_LNP = (55, 58)
AT_ADD = (56, 58)
BP = 4
CBK = 10
SINIT = 3
FFN_WEIGHTS = ("w1T", "w2T", "h1T", "h2T", "w3T")
PIECE, RING = 2 * DH, 4
RAW_ROWS = 128


def since_slot(k):
    return next(n for n in range(1, STEPS) if SLOT[(k - n) % STEPS] == SLOT[k])


class Chunk:

    def __init__(self, ps, c, d):
        self.ps, self.c, self.d = ps, c, d
        self.batch = d % BATCH
        self.step = c + d // BATCH if isinstance(c, int) else c + (d // BATCH)

    def go(self, k):
        return Chunk(self.ps, self.c, self.d + k)

    def number(self):
        return BATCH * self.c + self.d if isinstance(self.c, int) else None

    def first(self):
        return self.number() == 0

    def last(self):
        return self.number() == NCH - 1

    def at(self, per_chunk, off):
        return self.c * (BATCH * per_chunk) + (per_chunk * (NCH * self.ps + self.d) + off)

    def time(self, reverse):
        k = self.d // BATCH
        return (self.c * -1) + (NC - 1 - k) if reverse else self.c + k


def wait(eng, sem, value):
    if not (isinstance(value, int) and value <= 0):
        eng.wait_ge(sem, value)


def adaln_mamba_ffn(nc, a, out, yb_dram, x1_dram, xn_dram, b_dram, w_raw):
    x_v = a["x"].rearrange("b (c s p) d -> b c p s d", s=TS, p=P)
    yb_v = yb_dram.rearrange("b (c s p) d -> b c p s d", s=TS, p=P)
    x1_v = x1_dram.rearrange("b (c s p) d -> b c p s d", s=TS, p=P)
    xn_v = xn_dram.rearrange("b (c s p) d -> b c p s d", s=TS, p=P)
    out_v = out.rearrange("b (c s p) d -> b c p s d", s=TS, p=P)

    with ExitStack() as ctx:
        def sem(name):
            return ctx.enter_context(nc.semaphore(name))

        def sbuf(c, name, shape, dt=F32):
            return c.enter_context(nc.sbuf_tensor(name, shape, dt))

        bank = [ctx.enter_context(nc.psum_tensor(f"bank{i}", [P, T], F32)) for i in range(8)]

        ident = sbuf(ctx, "ident", [P, P])
        cols = sbuf(ctx, "cols", [P, 2, NCOL])
        mod = sbuf(ctx, "mod", [P, 12, BATCH])
        gain = sbuf(ctx, "gain", [P, 4, BATCH, DM])
        norm_c = sbuf(ctx, "norm_c", [P, 2, TS])
        fcol = sbuf(ctx, "fcol", [P, 4, KH])
        any_odd = sbuf(ctx, "any_odd", [1, 1], I32)

        s_raw = sem("w_raw")
        setup(nc, sbuf, a, bank, ident, cols, mod, gain, norm_c, fcol, any_odd)
        S = {n: sem(n) for n in SEM_NAMES}
        for ps in range(2):
            mamba_pass(nc, ps, a, bank, ident, cols, mod, gain, norm_c, x_v, yb_v, x1_v, xn_v, b_dram, w_raw, s_raw, S)
        ffn(nc, sem, sbuf, bank, ident, mod, gain, norm_c, fcol, any_odd, w_raw, s_raw, x1_v, out_v)


SEM_NAMES = [
    "w_in", "init", "go", "x_in", "ln", "fill0", "fill1", "fill2", "drain0", "drain1", "drain2", "halo", "xi", "z", "sp_exp", "sp_ln",
    "dt_done", "u_ready", "b_st", "b_in0", "b_in1", "da", "dbx", "scan", "save", "ht_fill", "stt", "gate", "y_out",
    "yb_in", "xr_in", "xnr_in", "xn_in", "xn_out", "comb",
]


def setup(nc, sbuf, a, bank, ident, cols, mod, gain, norm_c, fcol, any_odd):
    with ExitStack() as c:
        ct = sbuf(c, "ct", [P, KM, BATCH])
        cs = sbuf(c, "cs", [P, KM, BATCH])
        cbc = sbuf(c, "cbc", [P, KM, BATCH, P])
        wmod = sbuf(c, "wmod", [P, KM, 6 * DM])
        lng = sbuf(c, "lng", [P, 3, DM])
        rows = sbuf(c, "rows", [P, BATCH, 6, DM])
        ones = sbuf(c, "ones", [P, P])
        sgn = sbuf(c, "sgn", [P, BATCH, DM])
        mag = sbuf(c, "mag", [P, BATCH, DM])
        t0 = sbuf(c, "t0", [P, BATCH, DM])
        pieces = []
        for name in FFN_WEIGHTS:
            rows_p = PIECE // a[name].shape[1] * P
            for r in range(0, a[name].shape[0], rows_p):
                pieces.append(a[name][r:r + rows_p].rearrange("(p k) n -> p (k n)", p=P))
        wp = sbuf(c, "wp", [P, RING, PIECE])
        wr = sbuf(c, "wr", [P, 2, PIECE], F32R)
        wd = sbuf(c, "wd", [P, 2, PIECE])
        odd = sbuf(c, "odd", [P, len(pieces)])
        odd_sum = sbuf(c, "odd_sum", [1, 1])
        p_in = [c.enter_context(nc.semaphore(f"s_p_in{i}")) for i in range(RING)]
        s_round, s_diff, s_odd = (c.enter_context(nc.semaphore(n)) for n in ("s_round", "s_diff", "s_odd"))
        s_in, s_pool, s_silu, s_v, s_pe, s_a = (c.enter_context(nc.semaphore(n)) for n in
                                                ("s_in", "s_pool", "s_silu", "s_v", "s_pe", "s_a"))
        block = c.enter_context(nc.Block())

        @block.sync
        def _(sp):
            sp.dma_start(ct[:, :, :], a["cT"].rearrange("(k p) b -> p k b", p=P)).then_inc(s_in, 16)
            sp.dma_start(wmod[:, :, :], a["wmod"].rearrange("(k p) n -> p k n", p=P)).then_inc(s_in, 16)
            sp.dma_start(cols[:, 0, :], a["b_cols"]).then_inc(s_in, 16)
            sp.dma_start(cols[:, 1, :], a["f_cols"]).then_inc(s_in, 16)
            sp.dma_start(fcol[:, :, :], a["ffn_cols"]).then_inc(s_in, 16)
            for i, name in enumerate(("ln_g", "ln_b", "w3_s")):
                sp.dma_start(lng[:, i, :], a[name].partition_broadcast(P)).then_inc(s_in, 16)
            for n, piece in enumerate(pieces):
                wait(sp, s_diff, n - RING + 1)
                sp.dma_start(wp[:, n % RING, :], piece).then_inc(p_in[n % RING], 16)

        @block.gpsimd
        def _(pool):
            pool.memset(ident[:, :], 0.0).then_inc(s_pool, 1)
            pool.memset(norm_c[:, 0, :], EPS)
            pool.memset(norm_c[:, 1, :], -0.5)
            pool.memset(ones[:, :], 1.0).then_inc(s_pool, 1)
            pool.wait_ge(s_pool, 2)
            pool.affine_select(out=ident[:, :], in_=ident[:, :], compare_op=ALU.not_equal, fill=1.0, base=0,
                               pattern=[[-1, P]], channel_multiplier=1).then_inc(s_pool, 1)
            for n in range(len(pieces)):
                pool.wait_ge(s_round, n + 1)
                wait(pool, s_odd, n - 1)
                pool.tensor_tensor(wd[:, n % 2, :], wp[:, n % RING, :], wr[:, n % 2, :].bitcast(F32), ALU.subtract
                                   ).then_inc(s_diff, 1)

        @block.scalar
        def _(act):
            act.wait_ge(s_in, 128)
            act.activation(cs[:, :, :], ct[:, :, :], ACT.Silu).then_inc(s_silu, 1)
            for d in range(2):
                act.activation(cols[:, d, COL_A:], cols[:, d, COL_A:], ACT.Exp).then_inc(s_a, 1)

            def sum_odd(n):
                act.wait_ge(s_diff, n + 1)
                act.activation(wd[:, n % 2, :], wd[:, n % 2, :], ACT.Abs, accum_out=odd[:, n:n + 1]).then_inc(s_odd, 1)

            for n in range(len(pieces)):
                act.wait_ge(p_in[n % RING], 16 * (n // RING + 1))
                wait(act, s_diff, n - 1)
                act.copy(wr[:, n % 2, :], wp[:, n % RING, :]).then_inc(s_round, 1)
                if n:
                    sum_odd(n - 1)
            sum_odd(len(pieces) - 1)

        @block.tensor
        def _(pe):
            pe.wait_ge(s_silu, 1)
            for j in range(12):
                for k in range(KM):
                    last = pe.matmul(bank[0][:, 2 * j:2 * j + 2], wmod[:, k, j * P:(j + 1) * P], cs[:, k, :],
                                     start=(k == 0), stop=(k == KM - 1))
            last.then_inc(s_pe, 1)
            pe.wait_ge(s_v, 1)
            for b in range(BATCH):
                for j in range(3):
                    for k in range(KM):
                        last = pe.matmul(bank[1 + 3 * b + j][:, :], cbc[:, k, b, :],
                                         wmod[:, k, 2 * j * DM:2 * (j + 1) * DM], start=(k == 0), stop=(k == KM - 1))
            last.then_inc(s_pe, 1)
            pe.wait_ge(s_odd, len(pieces))
            pe.matmul(bank[7][0:1, 0:len(pieces)], ones[:, 0:1], odd[:, :], start=True, stop=True).then_inc(s_pe, 1)

        @block.vector
        def _(dve):
            n = [0]

            def step(ins):
                n[0] += 1
                ins.then_inc(s_v, 1)
                dve.wait_ge(s_v, n[0])

            dve.wait_ge(s_silu, 1)
            dve.wait_ge(s_pool, 2)
            for k in range(KM):
                for b in range(BATCH):
                    last = dve.tensor_scalar(cbc[:, k, b, :], ones[:, :], cs[:, k, b:b + 1], None, ALU.mult)
            step(last)
            dve.wait_ge(s_a, 2)
            step(dve.tensor_scalar(cols[:, :, COL_A:], cols[:, :, COL_A:], -1.0, None, ALU.mult))
            dve.wait_ge(s_pe, 1)
            step(dve.tensor_copy(mod[:, :, :], bank[0][:, 0:24].rearrange("p (j b) -> p j b", b=BATCH)))
            for part in (1, 4):
                m = mod[:, 2 * part:2 * part + 2, :]
                step(dve.tensor_scalar(m, m, 1.0, None, ALU.add))
            dve.wait_ge(s_pe, 2)
            for b in range(BATCH):
                for j in range(3):
                    step(dve.tensor_copy(rows[:, b, 2 * j:2 * j + 2, :],
                                         bank[1 + 3 * b + j][:, :].rearrange("p (g n) -> p g n", g=2)))
            for part in (2, 5):
                g = rows[:, :, part, :]
                step(dve.tensor_scalar(sgn[:, :, :], g, 0.0, 2.0, ALU.is_ge, ALU.mult))
                step(dve.tensor_scalar(sgn[:, :, :], sgn[:, :, :], -1.0, None, ALU.add))
                step(dve.tensor_scalar(mag[:, :, :], g, -1.0, 0.25, ALU.mult, ALU.max))
                step(dve.tensor_tensor(mag[:, :, :], mag[:, :, :], g, ALU.max))
                step(dve.tensor_tensor(g, sgn[:, :, :], mag[:, :, :], ALU.mult))
            for b in range(BATCH):
                ga, gb = rows[:, b, 2, :], rows[:, b, 5, :]
                step(dve.scalar_tensor_tensor(out=gain[:, 0, b, :], in0=ga, scalar=0.25, in1=lng[:, 0, :],
                                              op0=ALU.mult, op1=ALU.mult))
                step(dve.tensor_scalar(t0[:, b, :], rows[:, b, 1, :], 1.0, None, ALU.add))
                step(dve.tensor_tensor(gain[:, 1, b, :], ga, t0[:, b, :], ALU.mult))
                step(dve.tensor_tensor(t0[:, b, :], rows[:, b, 0, :], lng[:, 1, :], ALU.add))
                step(dve.tensor_tensor(gain[:, 2, b, :], ga, t0[:, b, :], ALU.mult))
                step(dve.tensor_tensor(gain[:, 3, b, :], gb, lng[:, 2, :], ALU.mult))
            dve.wait_ge(s_pe, 3)
            step(dve.tensor_reduce(odd_sum[:, :], bank[7][0:1, 0:len(pieces)], mybir.AxisListType.X, ALU.add))
            step(dve.tensor_scalar(odd_sum[:, :], odd_sum[:, :], 0.0, None, ALU.not_equal))
            step(dve.tensor_copy(any_odd[:, :], odd_sum[:, :]))


def mamba_pass(nc, ps, a, bank, ident, cols, mod, gain, norm_c, x_v, yb_v, x1_v, xn_v, b_dram, w_raw, s_raw, S):
    reverse = ps == 0
    w = "b_" if reverse else "f_"
    FB, DA, HT = bank[0:NFB], bank[NFB:NFB + NDA], bank[NFB + NDA:]
    flip = slice(None, None, -1) if reverse else slice(None)
    END = 0 if reverse else T - 1
    fill, drain = [S[f"fill{i}"] for i in range(NFB)], [S[f"drain{i}"] for i in range(NFB)]
    b_in = (S["b_in0"], S["b_in1"])

    with ExitStack() as c:
        def sb(name, shape):
            return c.enter_context(nc.sbuf_tensor(f"{w}{name}", shape, F32))

        w_in = sb("w_in", [P, KM, 2 * DI])
        w_x = sb("w_x", [P, KI, DTR + 2 * DS])
        w_dt = sb("w_dt", [DTR, DI])
        w_out = sb("w_out", [P, KI, DM])
        diag = sb("diag", [P, KI * DCONV, P])
        xn = sb("xn", [P, TS, DM])
        if reverse:
            xin = sb("xin", [P, TS, DM])
            stat = sb("stat", [P, TS, 6])
            mv = sb("mv", [P, TS, 4])
        hT = sb("hT", [P, KM, T])
        xpre = sb("xpre", [P, KI, T + HALO])
        halo = sb("halo", [P, BATCH, KI, HALO])
        xi = sb("xi", [P, BATCH, KI, T])
        z = sb("z", [P, BATCH, KI, T])
        dt = sb("dt", [P, BATCH, KI, T])
        u = sb("u", [P, BATCH, KI, T])
        dbB = sb("dbB", [P, T])
        Ct = sb("Ct", [P, BATCH, TS, DS])
        Bs = sb("Bs", [P, 2, BP, T])
        dBx = sb("dBx", [P, 2, KI, T])
        h = sb("h", [P, 2, KI, T])
        state = sb("state", [P, BATCH, DS, KI])
        acc = sb("acc", [P, BATCH, TS, DI])
        ysb = sb("ysb", [P, BATCH, TS, DM])
        if not reverse:
            ybt = sb("ybt", [P, TS, DM])
            xres = sb("xres", [P, TS, DM])
            dst = sb("dst", [P, TS, 6])
            dmv = sb("dmv", [P, TS, 4])
            xnres = sb("xnres", [P, TS, DM])
        block = c.enter_context(nc.Block())
        cv = cols[:, ps, :]

        def job(ch, i):
            b = BANK[i]
            front_jobs, tail_jobs = ([k for k in jobs if BANK[k] == b] for jobs in (FRONT, TAIL))
            nf, nt = len(front_jobs), len(tail_jobs)
            fronts_before, tails_before = (sum(k < i for k in jobs) for jobs in (front_jobs, tail_jobs))
            if i in TAIL:
                if ch.number() is not None and ch.number() >= NCH - 2:
                    n = ch.number() * nt + tails_before + NCH * nf
                    return b, n + ps * NCH * (nf + nt)
                return b, ch.at(nf + nt, tails_before + 2 * nf + fronts_before)
            if ch.number() is not None and ch.number() < 2:
                return b, ch.number() * nf + fronts_before + ps * NCH * (nf + nt)
            return b, ch.at(nf + nt, fronts_before - 2 * nt + tails_before)

        def wait_filled(eng, ch, i):
            b, k = job(ch, i)
            eng.wait_ge(fill[b], k + 1)

        def wait_drained(eng, ch, i):
            b, k = job(ch, i)
            eng.wait_ge(drain[b], k + 1)

        def wait_free(eng, ch, i):
            b, k = job(ch, i)
            wait(eng, drain[b], k)

        def schedule(eng, body, flush, prologue):
            prologue(Chunk(ps, 0, 0))
            for d in range(BATCH):
                body(Chunk(ps, 0, d))
            with eng.Fori(1, NC - 1) as c:
                for d in range(BATCH):
                    body(Chunk(ps, c, d))
            for d in range(BATCH):
                body(Chunk(ps, NC - 1, d))
            flush(Chunk(ps, NC - 1, 1))

        def has(ch, k):
            return ch.number() is None or 0 <= ch.number() + k < NCH

        @block.sync
        def _(sp):
            for dst, src in ((w_in[:, :, :], a[w + "in_projT"].rearrange("(k p) n -> p k n", p=P)),
                             (w_x[:, :, :], a[w + "x_projT"].rearrange("(k p) n -> p k n", p=P)),
                             (w_dt[:, :], a[w + "dt_wT"]),
                             (w_out[:, :, :], a[w + "out_projT"].rearrange("(k p) n -> p k n", p=P))):
                sp.dma_start(dst, src).then_inc(S["w_in"], 16)

            def load_x(ch):
                if not reverse:
                    if not ch.first():
                        wait_filled(sp, ch.go(-1), J_LN[1])
                        sp.sem_inc(S["go"], 1)
                    sp.dma_start(xn[:, :, :], xn_v[ch.batch, ch.time(False)]).then_inc(S["xn_in"], 16)
                    return
                wait(sp, S["ln"], ch.at(LNK, 0))
                sp.dma_start(xin[:, :, :], x_v[ch.batch, ch.time(reverse)]).then_inc(S["x_in"], 16)

            def store_xn(ch):
                sp.wait_ge(S["ln"], ch.at(LNK, LNK))
                sp.dma_start(xn_v[ch.batch, ch.time(True)], xn[:, :, :]).then_inc(S["xn_out"], 16)

            def store_b(ch):
                wait_drained(sp, ch, J_B)
                sp.dma_start(b_dram[ch.batch], dbB[B0:B0 + DS, :]).then_inc(S["b_st"], 16)

            def load_b(ch, j):
                wait(sp, S["dbx"], ch.at(2 * DS, 2 * BP * (j - 1)))
                if j == 0:
                    sp.sem_inc(S["go"], 1)
                    sp.wait_ge(S["b_st"], ch.at(16, 16))
                sp.dma_start(Bs[:, j % 2, :, :], b_dram[ch.batch, BP * j:BP * (j + 1), :].partition_broadcast(P)
                             ).then_inc(b_in[j % 2], 16)

            def load_join(ch):
                f = Chunk(0, ch.c, ch.d)
                wait(sp, S["comb"], f.at(CBK, 0))
                sp.dma_start(ybt[:, :, :], yb_v[ch.batch, ch.time(False)]).then_inc(S["yb_in"], 16)
                sp.dma_start(xres[:, :, :], x_v[ch.batch, ch.time(False)]).then_inc(S["xr_in"], 16)
                sp.dma_start(xnres[:, :, :], xn_v[ch.batch, ch.time(False)]).then_inc(S["xnr_in"], 16)

            def store_x1(ch):
                sp.wait_ge(S["comb"], Chunk(0, ch.c, ch.d).at(CBK, CBK))
                sp.dma_start(x1_v[ch.batch, ch.time(False)], ysb[:, ch.batch, :, :]).then_inc(S["y_out"], 16)

            def store_y(ch):
                wait_drained(sp, ch, J_OUT[1])
                sp.dma_start(yb_v[ch.batch, ch.time(True)], ysb[:, ch.batch, :, :]).then_inc(S["y_out"], 16)

            def prologue(ch):
                load_x(ch)
                if reverse:
                    store_xn(ch)
                load_x(ch.go(1))
                if reverse:
                    store_xn(ch.go(1))
                store_b(ch)
                load_b(ch, 0)
                load_b(ch, 1)

            def body(ch):
                if has(ch, 2):
                    load_x(ch.go(2))
                load_b(ch, 2)
                load_b(ch, 3)
                if not reverse:
                    if has(ch, -2):
                        store_x1(ch.go(-2))
                    if has(ch, -1):
                        load_join(ch.go(-1))
                if reverse and has(ch, 2):
                    store_xn(ch.go(2))
                if has(ch, 1):
                    store_b(ch.go(1))
                    load_b(ch.go(1), 0)
                if reverse and has(ch, -1):
                    store_y(ch.go(-1))
                if has(ch, 1):
                    load_b(ch.go(1), 1)

            def flush(ch):
                if reverse:
                    store_y(ch)
                    sp.wait_ge(S["xn_out"], 16 * NCH)
                else:
                    store_x1(ch.go(-1))
                    load_join(ch)
                    store_x1(ch)
                sp.wait_ge(S["y_out"], ch.at(16, 16))

            schedule(sp, body, flush, prologue)

        @block.tensor
        def _(pe):
            def turn(i, src, m, ch):
                wait_free(pe, ch, i)
                for s in range(TS):
                    mm = pe.transpose(FB[BANK[i]][:, s * P:(s + 1) * P], src(s), ident[:, :])
                mm.then_inc(fill[BANK[i]], 1)

            def part(ch, i, k, kn, lhsT, rhs, rows=P):
                if k == 0:
                    wait_free(pe, ch, i)
                mm = pe.matmul(FB[BANK[i]][0:rows, :], lhsT, rhs, start=(k == 0), stop=(k == kn - 1))
                if k == kn - 1:
                    mm.then_inc(fill[BANK[i]], 1)

            def front(ch, g):
                q = ch.batch
                for k in range(KM):
                    if g == AT_LN[k]:
                        if k == 0:
                            if reverse:
                                pe.wait_ge(S["ln"], ch.at(LNK, LNK))
                            else:
                                pe.wait_ge(S["xn_in"], Chunk(0, ch.c, ch.d).at(16, 16))
                        turn(J_LN[k], lambda s: xn[:, s, k * P:(k + 1) * P], k, ch)
                for m in range(KI):
                    k = g - AT_X[m]
                    if 0 <= k < KM:
                        if m == 0:
                            wait_drained(pe, ch, J_LN[k])
                        part(ch, J_X[m], k, KM, w_in[:, k, m * P:(m + 1) * P], hT[:, k, :])
                    k = g - AT_CONV[m]
                    if 0 <= k < DCONV:
                        if k == 0:
                            if m == 0:
                                pe.wait_ge(S["halo"], ch.at(2, 1))
                            if BANK[J_X[m]] != BANK[J_CONV[m]]:
                                wait_drained(pe, ch, J_X[m])
                        o = HALO - k if reverse else k
                        part(ch, J_CONV[m], k, DCONV, diag[:, m * DCONV + k, :], xpre[:, m, o:o + T])
                    if g == AT_DT[m]:
                        if m == 0:
                            wait_drained(pe, ch, J_B)
                        part(ch, J_DT[m], 0, 1, w_dt[:, m * P:(m + 1) * P], dbB[0:DTR, :])
                    k = g - AT_Z[m]
                    if 0 <= k < KM:
                        part(ch, J_Z[m], k, KM, w_in[:, k, (KI + m) * P:(KI + m + 1) * P], hT[:, k, :])
                    if g == AT_B + m:
                        pe.wait_ge(S["xi"], ch.at(KI, m + 1))
                        part(ch, J_B, m, KI, w_x[:, m, 0:B0 + DS], xi[:, q, m, :], B0 + DS)
                for half in range(2):
                    if g == AT_C + half:
                        if half == 0:
                            wait_free(pe, ch, J_C)
                        for s in (2 * half, 2 * half + 1):
                            for k in range(KI):
                                mm = pe.matmul(FB[BANK[J_C]][:, s * DS:(s + 1) * DS], xi[:, q, k, s * P:(s + 1) * P],
                                               w_x[:, k, B0 + DS:], start=(k == 0), stop=(k == KI - 1))
                        if half == 1:
                            mm.then_inc(fill[BANK[J_C]], 1)

            def tail(ch, g):
                q = ch.batch
                for m in range(KI):
                    if g == AT_Y[m]:
                        if m == 0:
                            pe.wait_ge(S["stt"], ch.at(STEPS, STEPS))
                        turn(J_Y[m], lambda s: acc[:, q, s, m * P:(m + 1) * P], m, ch)
                for i in range(2):
                    r = g - AT_OUT[i]
                    if 0 <= r < 4:
                        if r == 0:
                            if i == 0:
                                pe.wait_ge(S["gate"], ch.at(2, 2))
                            wait_free(pe, ch, J_OUT[i])
                        s = 2 * i + r // 2
                        for k in (0, 1) if r % 2 == 0 else (2, 3):
                            mm = pe.matmul(FB[BANK[J_OUT[i]]][:, (r // 2) * DM:(r // 2 + 1) * DM], z[:, q, k, s * P:(s + 1) * P],
                                           w_out[:, k, :], start=(k == 0), stop=(k == KI - 1))
                        if r == 3:
                            mm.then_inc(fill[BANK[J_OUT[i]]], 1)

            def turn_h(ch, s, t):
                if t == 0:
                    pe.wait_ge(S["scan"], ch.at(STEPS, KI * (s + 1)))
                wait(pe, S["stt"], ch.at(STEPS, TS * s + t - 1))
                for m in range(KI):
                    mm = pe.transpose(HT[t % 2][:, m * P:(m + 1) * P], h[:, s % 2, m, t * P:(t + 1) * P], ident[:, :])
                mm.then_inc(S["ht_fill"], 1)

            def body(ch):
                for s in range(DS):
                    for t in range(TS):
                        if s:
                            turn_h(ch, s - 1, t)
                        elif has(ch, -1):
                            turn_h(ch.go(-1), DS - 1, t)
                        if has(ch, -1):
                            tail(ch.go(-1), TS * s + t)
                        if has(ch, 1):
                            front(ch.go(1), TS * s + t)

            def prologue(ch):
                pe.wait_ge(S["w_in"], 64 * (ps + 1))
                pe.wait_ge(S["init"], SINIT * (ps + 1))
                for g in range(STEPS):
                    front(ch, g)

            def flush(ch):
                for t in range(TS):
                    turn_h(ch, DS - 1, t)
                for g in range(STEPS):
                    tail(ch, g)

            schedule(pe, body, flush, prologue)

        @block.scalar
        def _(act):
            def front(ch, g):
                q = ch.batch
                g -= ACT_LAG
                for k in range(KM):
                    if g == AT_LN[k]:
                        wait_filled(act, ch, J_LN[k])
                        act.activation(hT[:, k, :], FB[BANK[J_LN[k]]][:, :], ACT.Identity, bias=mod[:, k, q:q + 1],
                                       scale=mod[:, 2 + k, q:q + 1]).then_inc(drain[BANK[J_LN[k]]], 1)
                lo = 0 if reverse else HALO
                for m in range(KI):
                    if g == AT_X[m] + KM - 1:
                        if m == 0:
                            wait(act, S["halo"], ch.at(2, -2))
                            act.wait_ge(S["init"], SINIT * (ps + 1))
                            act.copy(xpre[:, :, T:] if reverse else xpre[:, :, 0:HALO],
                                     halo[:, q, :, :]).then_inc(S["halo"], 1)
                        wait_filled(act, ch, J_X[m])
                        act.copy(xpre[:, m, lo:lo + T], FB[BANK[J_X[m]]][:, :]).then_inc(drain[BANK[J_X[m]]], 1)
                        if m == KI - 1:
                            for i in (KI - 2, KI - 1):
                                wait_drained(act, ch, J_X[i])
                            act.wait_ge(S["halo"], ch.at(2, 1))
                            act.copy(halo[:, q, :, :], xpre[:, :, 0:HALO] if reverse else xpre[:, :, T:]
                                     ).then_inc(S["halo"], 1)
                    if g == AT_CONV[m] + DCONV - 1:
                        wait_filled(act, ch, J_CONV[m])
                        b = BANK[J_CONV[m]]
                        act.activation(u[:, q, m, :], FB[b][:, :], ACT.Identity,
                                       bias=cv[:, COL_CB + m:COL_CB + m + 1]).then_inc(drain[b], 1)
                    if g == AT_Z[m] + KM - 1:
                        wait_filled(act, ch, J_Z[m])
                        b = BANK[J_Z[m]]
                        act.copy(z[:, q, m, :], FB[b][:, :]).then_inc(drain[b], 1)
                if g == AT_B + KI - 1:
                    wait(act, S["b_st"], ch.at(16, 0))
                    wait_filled(act, ch, J_B)
                    act.copy(dbB[0:B0 + DS, :], FB[BANK[J_B]][0:B0 + DS, :]).then_inc(drain[BANK[J_B]], 1)
                if g == AT_C + 1:
                    wait(act, S["stt"], ch.at(STEPS, -STEPS))
                    wait_filled(act, ch, J_C)
                    act.copy(Ct[:, q, :, :], FB[BANK[J_C]][:, 0:TS * DS].rearrange("p (t s) -> p t s", s=DS)
                             ).then_inc(drain[BANK[J_C]], 1)
                for m in range(KI):
                    if g == AT_DT[m]:
                        wait_filled(act, ch, J_DT[m])
                        bias = cv[:, COL_DTB + m:COL_DTB + m + 1]
                        b = BANK[J_DT[m]]
                        act.activation(u[:, q, m, :], FB[b][:, :], ACT.Abs, bias=bias)
                        act.activation(dt[:, q, m, :], FB[b][:, :], ACT.Relu, bias=bias).then_inc(drain[b], 1)
                for half in range(2):
                    m = 2 * half
                    o = u[:, q, m:m + 2, :]
                    if g + ACT_LAG == AT_EXP[half]:
                        for i in (m, m + 1):
                            wait_drained(act, ch, J_DT[i])
                        act.activation(o, o, ACT.Exp, scale=-1.0).then_inc(S["sp_exp"], 1)
                    if g + ACT_LAG == AT_LNP[half]:
                        act.wait_ge(S["sp_exp"], ch.at(2, half + 1))
                        act.activation(o, o, ACT.Ln, bias=1.0).then_inc(S["sp_ln"], 1)

            def silu(ch, g):
                for m in range(KI):
                    if g == AT_SILU[m]:
                        if has(ch, 1):
                            xi_silu(ch.go(1), m)
                        wait_drained(act, ch, J_Z[m])
                        o = z[:, ch.batch, m, :]
                        act.activation(o, o, ACT.Silu).then_inc(S["z"], 1)

            def xi_silu(ch, m):
                if m == 0:
                    wait(act, S["gate"], ch.at(2, -2))
                wait_drained(act, ch, J_CONV[m])
                act.activation(xi[:, ch.batch, m, :], u[:, ch.batch, m, :], ACT.Silu).then_inc(S["xi"], 1)

            def tail(ch, g):
                for i in range(2):
                    if g == AT_OUT[i] + 3 + ACT_LAG:
                        if i == 0:
                            wait(act, S["y_out"], ch.at(16, -16))
                        wait_filled(act, ch, J_OUT[i])
                        b = BANK[J_OUT[i]]
                        act.activation(ysb[:, ch.batch, 2 * i:2 * i + 2, :], FB[b][:, :].rearrange("p (s n) -> p s n", s=2),
                                       ACT.Tanh, scale=0.5).then_inc(drain[b], 1)

            def decay(ch, k):
                s, m = divmod(k, KI)
                if k == 0:
                    act.wait_ge(S["dt_done"], ch.at(2, 2))
                wait(act, S["scan"], ch.at(STEPS, k - since_slot(k) + 1))
                col = COL_A + m * DS + s
                act.activation(DA[SLOT[k]][:, :], dt[:, ch.batch, m, :], ACT.Exp, scale=cv[:, col:col + 1]
                               ).then_inc(S["da"], 1)

            copies = [(w_raw[name][r:r + RAW_ROWS], a[name][r:r + RAW_ROWS]) for name in w_raw
                      for r in range(0, a[name].shape[0], RAW_ROWS)]

            def body(ch):
                for k in range(STEPS):
                    decay(ch, k)
                    if reverse and ch.first() and k % 2 == 0 and k // 2 < len(copies):
                        act.dma_start(*copies[k // 2]).then_inc(s_raw, 16)
                    front(ch, STEPS + k)
                    if has(ch, -1):
                        tail(ch.go(-1), k)
                    if has(ch, 1):
                        front(ch.go(1), k)
                    silu(ch, k)

            def prologue(ch):
                for g in range(STEPS):
                    front(ch, g)
                    for m in range(KI):
                        if g == AT_SILU[m]:
                            xi_silu(ch, m)

            def flush(ch):
                for g in range(STEPS):
                    tail(ch, g)

            schedule(act, body, flush, prologue)

        @block.gpsimd
        def _(pool):
            def norm(ch):
                pool.wait_ge(S["ln"], ch.at(LNK, 2))
                pool.tensor_tensor(mv[:, :, 2], mv[:, :, 1], norm_c[:, 0, :], ALU.add).then_inc(S["ln"], 1)
                pool.wait_ge(S["ln"], ch.at(LNK, 3))
                pool.tensor_tensor(mv[:, :, 3], mv[:, :, 2], norm_c[:, 1, :], ALU.pow).then_inc(S["ln"], 1)

            def make_u(ch, half):
                q = ch.batch
                m = slice(2 * half, 2 * half + 2)
                pool.wait_ge(S["dt_done"], ch.at(2, half + 1))
                pool.tensor_tensor(u[:, q, m, :], dt[:, q, m, :], xi[:, q, m, :], ALU.mult).then_inc(S["u_ready"], 1)

            def gate(ch, half):
                q = ch.batch
                m = slice(2 * half, 2 * half + 2)
                if half == 0:
                    pool.wait_ge(S["z"], ch.at(KI, KI))
                    for i in (KI - 2, KI - 1):
                        wait_drained(pool, ch, J_Y[i])
                pool.tensor_tensor(z[:, q, m, :], z[:, q, m, :], xi[:, q, m, :], ALU.mult).then_inc(S["gate"], 1)

            def keep_state(ch, s):
                pool.wait_ge(S["scan"], ch.at(STEPS, KI * (s + 1)))
                pool.sem_inc(S["go"], 1)
                pool.tensor_copy(state[:, ch.batch, s, :], h[:, s % 2, :, END]).then_inc(S["save"], 1)

            def weigh_b(ch, s, half):
                m = slice(2 * half, 2 * half + 2)
                wait(pool, S["scan"], ch.at(STEPS, KI * (s - 2) + 2 * half + 2))
                pool.tensor_tensor(dBx[:, s % 2, m, :], u[:, ch.batch, m, :],
                                   Bs[:, (s // BP) % 2, s % BP, :].unsqueeze(1).broadcast_to((P, 2, T)),
                                   ALU.mult).then_inc(S["dbx"], 1)

            def join(ch):
                f = Chunk(0, ch.c, ch.d)
                pool.wait_ge(S["comb"], f.at(CBK, 4))
                pool.tensor_tensor(dmv[:, :, 3], dmv[:, :, 2], norm_c[:, 1, :], ALU.pow).then_inc(S["comb"], 1)

            def body(ch):
                for s in range(DS):
                    if s % BP == 0:
                        j = s // BP
                        pool.wait_ge(b_in[j % 2], ch.at(32, 16 * (j // 2) + 16))
                    for half in range(2):
                        if s == 0:
                            if half == 1:
                                make_u(ch, 1)
                            pool.wait_ge(S["u_ready"], ch.at(2, half + 1))
                        if half == 1:
                            if s >= 2:
                                keep_state(ch, s - 2)
                            elif has(ch, -1):
                                keep_state(ch.go(-1), DS - 2 + s)
                        weigh_b(ch, s, half)
                        if s == GATE_S and has(ch, -1):
                            gate(ch.go(-1), half)
                    if s == 4 and not reverse and has(ch, -2):
                        join(ch.go(-2))
                    if reverse and s == NORM_S[1] + 2 and has(ch, 2):
                        norm(ch.go(2))
                    if s == DS - 1 and has(ch, 1):
                        make_u(ch.go(1), 0)

            def prologue(ch):
                if reverse:
                    norm(ch)
                    norm(ch.go(1))
                make_u(ch, 0)

            def flush(ch):
                for s in (DS - 2, DS - 1):
                    keep_state(ch, s)
                if not reverse:
                    join(ch.go(-1))
                for half in range(2):
                    gate(ch, half)
                if not reverse:
                    join(ch)

            schedule(pool, body, flush, prologue)

        @block.vector
        def _(dve):
            def norm(ch, slot):
                if slot == NORM_S[0]:
                    dve.wait_ge(S["x_in"], ch.at(16, 16))
                    wait(dve, S["ln"], ch.at(LNK, 0))
                    for s in range(TS):
                        ins = dve.bn_stats(stat[:, s, :], xin[:, s, :])
                    ins.then_inc(S["ln"], 1)
                if slot == NORM_S[1]:
                    dve.wait_ge(S["ln"], ch.at(LNK, 1))
                    dve.sem_inc(S["go"], 1)
                    for s in range(TS):
                        ins = dve.bn_aggr(mv[:, s, 0:2], stat[:, s, :])
                    ins.then_inc(S["ln"], 1)
                if slot == NORM_S[2]:
                    if not ch.first():
                        dve.wait_ge(S["xn_out"], ch.at(16, 0))
                        wait_filled(dve, ch.go(-1), J_LN[0])
                        wait_filled(dve, ch.go(-1), J_LN[1])
                    dve.wait_ge(S["ln"], ch.at(LNK, 4))
                    for s in range(TS):
                        ins = dve.tensor_scalar(xn[:, s, :], xin[:, s, :], mv[:, s, 0:1], mv[:, s, 3:4],
                                                ALU.subtract, ALU.mult)
                    ins.then_inc(S["ln"], 1)

            def front(ch, g):
                q = ch.batch
                for half in range(2):
                    m = 2 * half
                    if g == AT_ADD[half]:
                        for i in (m, m + 1):
                            wait_drained(dve, ch, J_DT[i])
                        dve.wait_ge(S["sp_ln"], ch.at(2, half + 1))
                        dve.tensor_tensor(dt[:, q, m:m + 2, :], dt[:, q, m:m + 2, :], u[:, q, m:m + 2, :], ALU.add
                                          ).then_inc(S["dt_done"], 1)

            def tail(ch, g):
                q = ch.batch
                for m in range(KI):
                    if g == AT_Y[m] + DVE_LAG:
                        wait_filled(dve, ch, J_Y[m])
                        dve.scalar_tensor_tensor(out=xi[:, q, m, :], in0=xi[:, q, m, :],
                                                 scalar=cv[:, COL_D + m:COL_D + m + 1], in1=FB[BANK[J_Y[m]]][:, :],
                                                 op0=ALU.mult, op1=ALU.add).then_inc(drain[BANK[J_Y[m]]], 1)

            def join(ch, slot):
                q = ch.batch
                y = ysb[:, q, :, :]
                f = Chunk(0, ch.c, ch.d)

                def after(k):
                    dve.wait_ge(S["comb"], f.at(CBK, k))

                def gains(i):
                    return gain[:, i, q, :].unsqueeze(1).broadcast_to((P, TS, DM))

                if slot == 0:
                    wait_drained(dve, ch, J_OUT[0])
                    wait_drained(dve, ch, J_OUT[1])
                    dve.wait_ge(S["yb_in"], f.at(16, 16))
                    dve.tensor_tensor(y, y, ybt[:, :, :], ALU.add).then_inc(S["comb"], 1)
                if slot == 1:
                    after(1)
                    for s in range(TS):
                        ins = dve.bn_stats(dst[:, s, :], y[:, s, :])
                    ins.then_inc(S["comb"], 1)
                if slot == 2:
                    after(2)
                    dve.sem_inc(S["go"], 1)
                    for s in range(TS):
                        ins = dve.bn_aggr(dmv[:, s, 0:2], dst[:, s, :])
                    ins.then_inc(S["comb"], 1)
                if slot == 3:
                    after(3)
                    dve.tensor_scalar(dmv[:, :, 2], dmv[:, :, 1], 1 / 16, EPS, ALU.mult, ALU.add).then_inc(S["comb"], 1)
                if slot == 5:
                    after(5)
                    for s in range(TS):
                        ins = dve.scalar_tensor_tensor(out=y[:, s, :], in0=y[:, s, :], scalar=dmv[:, s, 0:1],
                                                       in1=gain[:, 0, q, :], op0=ALU.subtract, op1=ALU.mult)
                    ins.then_inc(S["comb"], 1)
                if slot == 6:
                    after(6)
                    dve.wait_ge(S["xnr_in"], f.at(16, 16))
                    dve.tensor_tensor(ybt[:, :, :], xnres[:, :, :], gains(1), ALU.mult).then_inc(S["comb"], 1)
                if slot == 7:
                    after(7)
                    for s in range(TS):
                        ins = dve.scalar_tensor_tensor(out=y[:, s, :], in0=y[:, s, :], scalar=dmv[:, s, 3:4],
                                                       in1=ybt[:, s, :], op0=ALU.mult, op1=ALU.add)
                    ins.then_inc(S["comb"], 1)
                if slot == 8:
                    after(8)
                    dve.wait_ge(S["xr_in"], f.at(16, 16))
                    dve.tensor_tensor(y, y, xres[:, :, :], ALU.add).then_inc(S["comb"], 1)
                if slot == 9:
                    after(9)
                    dve.tensor_tensor(y, y, gains(2), ALU.add).then_inc(S["comb"], 1)

            def scan(ch, s, m):
                q = ch.batch
                k = KI * s + m
                if m == 0:
                    wait(dve, S["ht_fill"], ch.at(STEPS, TS * (s - 1)))
                    wait(dve, S["save"], ch.at(DS, s - 1))
                if m % 2 == 0:
                    dve.wait_ge(S["dbx"], ch.at(2 * DS, 2 * s + m // 2 + 1))
                dve.wait_ge(S["da"], ch.at(STEPS, k + 1))
                dve.tensor_tensor_scan(h[:, s % 2, m, flip], DA[SLOT[k]][:, flip], dBx[:, s % 2, m, flip],
                                       state[:, q, s, m:m + 1], ALU.mult, ALU.add).then_inc(S["scan"], 1)

            def weigh(ch, s, t):
                q = ch.batch
                dve.wait_ge(S["ht_fill"], ch.at(STEPS, TS * s + t + 1))
                scale = Ct[:, q, t, s:s + 1]
                if s == 0:
                    if t == 0:
                        wait_drained(dve, ch, J_C)
                    dve.tensor_scalar(acc[:, q, t, :], HT[t % 2][:, :], scale, None, ALU.mult).then_inc(S["stt"], 1)
                else:
                    dve.wait_ge(S["stt"], ch.at(STEPS, TS * (s - 1) + t + 1))
                    dve.scalar_tensor_tensor(out=acc[:, q, t, :], in0=HT[t % 2][:, :], scalar=scale,
                                             in1=acc[:, q, t, :], op0=ALU.mult, op1=ALU.add).then_inc(S["stt"], 1)

            def body(ch):
                for s in range(DS):
                    old = (ch, s - 1) if s else (ch.go(-1), DS - 1)
                    for m in range(KI):
                        scan(ch, s, m)
                        if s or has(ch, -1):
                            weigh(*old, m)
                        if has(ch, -1):
                            tail(ch.go(-1), KI * s + m)
                        if has(ch, 1):
                            front(ch.go(1), KI * s + m)
                    if not reverse and has(ch, -2):
                        join(ch.go(-2), s)
                    if reverse and has(ch, 2):
                        norm(ch.go(2), s)

            def prologue(ch):
                dve.wait_ge(S["w_in"], 64 * (ps + 1))
                for k in range(KI * DCONV):
                    ins = dve.tensor_scalar(diag[:, k, :], ident[:, :], cv[:, COL_CW + k:COL_CW + k + 1], None, ALU.mult)
                ins.then_inc(S["init"], 1)
                dve.memset(halo[:, :, :, :], 0.0).then_inc(S["init"], 1)
                dve.memset(state[:, :, :, :], 0.0).then_inc(S["init"], 1)
                dve.wait_ge(S["init"], SINIT * (ps + 1))
                if reverse:
                    for k in range(2):
                        for s in range(DS):
                            norm(ch.go(k), s)
                for g in range(STEPS):
                    front(ch, g)

            def flush(ch):
                for t in range(TS):
                    weigh(ch, DS - 1, t)
                for g in range(STEPS):
                    tail(ch, g)
                if not reverse:
                    for s in range(DS):
                        join(ch.go(-1), s)
                    for s in range(DS):
                        join(ch, s)

            schedule(dve, body, flush, prologue)


def ffn(nc, sem, sbuf, bank, ident, mod, gain, norm_c, fcol, any_odd, w_raw, s_raw, x1_v, out_v):
    F_12, F_H1, F_LN, F_H2, F_3 = 0, 2 * KH, 3 * KH, 3 * KH + KM, 4 * KH + KM
    FJOBS = F_3 + 2
    X_12, X_H1, X_LN, X_H2 = 0, KH, 2 * KH, 2 * KH + KM
    XTILES = 3 * KH + KM
    NBK = 6
    XR = 2
    FLN = 5
    with ExitStack() as c:
        w1 = sbuf(c, "w1", [P, KM, DH], F32R)
        w2 = sbuf(c, "w2", [P, KM, DH], F32R)
        h1 = sbuf(c, "h1", [P, KH, DH], F32R)
        h2 = sbuf(c, "h2", [P, KH, DH], F32R)
        w3 = sbuf(c, "w3", [P, KH, DM], F32R)
        x1 = sbuf(c, "x1", [P, BATCH, TS, DM])
        xn = sbuf(c, "xn2", [P, TS, DM])
        stat = sbuf(c, "stat2", [P, TS, 6])
        mv = sbuf(c, "mv2", [P, TS, 4])
        raw = sbuf(c, "raw", [P, XR, T])
        hT = sbuf(c, "hT2", [P, 2, KM, T], F32R)
        ga = sbuf(c, "ga", [P, 2, KH, T], F32R)
        gb = sbuf(c, "gb", [P, 2, KH, T], F32R)
        s1 = sbuf(c, "s1", [P, 2, T])
        ot = sbuf(c, "ot", [P, TS, DM])
        weights = ((w1, "w1T"), (w2, "w2T"), (h1, "h1T"), (h2, "h2T"), (w3, "w3T"))
        W_1, W_2, W_H1, W_H2, W_3 = range(len(weights))
        S = {n: c.enter_context(nc.semaphore("f_" + n)) for n in
             ("x_in0", "x_in1", "ln", "go", "fin", "o_out", "hi", "lo",
              *(f"w_in{i}" for i in range(len(weights))),
              *(f"fill{i}" for i in range(NBK)), *(f"drain{i}" for i in range(NBK)))}
        fill = [S[f"fill{i}"] for i in range(NBK)]
        drain = [S[f"drain{i}"] for i in range(NBK)]
        block = c.enter_context(nc.Block())

        def job(ch, i):
            if F_LN <= i < F_LN + KM:
                i = i - F_LN - KM if ch.first() else i - FJOBS
            elif ch.last() and i >= F_H2:
                i -= KM
            return (i + KM) % NBK, ch.at(FJOBS // NBK, (i + KM) // NBK)

        def tile(ch, j):
            if X_LN <= j < X_LN + KM:
                j = j - X_LN - KM if ch.first() else j - XTILES
            elif ch.last() and j >= X_H2:
                j -= KM
            return ch.at(XTILES, j + KM)

        def wait_filled(eng, ch, i):
            b, k = job(ch, i)
            eng.wait_ge(fill[b], k + 1)

        def wait_drained(eng, ch, i):
            b, k = job(ch, i)
            eng.wait_ge(drain[b], k + 1)

        def wait_free(eng, ch, i):
            b, k = job(ch, i)
            wait(eng, drain[b], k)

        def schedule(eng, body):
            for d in range(BATCH):
                body(Chunk(0, 0, d))
            with eng.Fori(1, NC - 1) as c:
                for d in range(BATCH):
                    body(Chunk(0, c, d))
            for d in range(BATCH):
                body(Chunk(0, NC - 1, d))

        @block.sync
        def _(sp):
            def load(ch):
                if ch.number() is None or ch.number() >= BATCH:
                    sp.wait_ge(S["fin"], ch.go(-BATCH).at(2, 2))
                sp.dma_start(x1[:, ch.batch, :, :], x1_v[ch.batch, ch.time(False)]).then_inc(S[f"x_in{ch.batch}"], 16)

            def body(ch):
                if not ch.last():
                    load(ch.go(1))
                sp.wait_ge(S["fin"], ch.at(2, 2))
                sp.sem_inc(S["go"], 1)
                sp.dma_start(out_v[ch.batch, ch.time(False)], ot[:, :, :]).then_inc(S["o_out"], 16)

            load(Chunk(0, 0, 0))
            sp.wait_ge(s_raw, 16 * sum(w.shape[0] // RAW_ROWS for w in w_raw.values()))
            for i, (dst, name) in enumerate(weights):
                sp.dma_start(dst[:, :, :].bitcast(F32), w_raw[name].rearrange("(k p) n -> p k n", p=P)
                             ).then_inc(S[f"w_in{i}"], 16)
            schedule(sp, body)
            sp.wait_ge(S["o_out"], 16 * NCH)

        @block.tensor
        def _(pe):
            def program(one_pass):
                def product(out, lhsT, rhs, start, stop):
                    if not one_pass:
                        lhsT, rhs = lhsT.bitcast(F32), rhs.bitcast(F32)
                    return pe.matmul(out, lhsT, rhs, start=start, stop=stop)

                def layer(ch, i, wt, m, src, kn, first_tile):
                    wait_free(pe, ch, i)
                    for k in range(kn):
                        if first_tile is not None:
                            pe.wait_ge(S["lo"], tile(ch, first_tile + k) + 1)
                        for half in range(2):
                            mm = product(bank[job(ch, i)[0]][:, :], wt[:, k, m * P:(m + 1) * P], src[:, half, k, :],
                                         k == 0 and half == 0, k == kn - 1 and half == 1)
                    mm.then_inc(fill[job(ch, i)[0]], 1)

                def turn(ch):
                    pe.wait_ge(S["ln"], ch.at(FLN, 5))
                    for k in range(KM):
                        b = job(ch, F_LN + k)[0]
                        wait_free(pe, ch, F_LN + k)
                        for s in range(TS):
                            mm = pe.transpose(bank[b][:, s * P:(s + 1) * P], xn[:, s, k * P:(k + 1) * P], ident[:, :])
                        mm.then_inc(fill[b], 1)

                def wait_weights(ch, i):
                    if ch.first():
                        pe.wait_ge(S[f"w_in{i}"], 16)

                def body(ch):
                    wait_weights(ch, W_1)
                    wait_weights(ch, W_2)
                    for m in range(KH):
                        layer(ch, F_12 + 2 * m, w1, m, hT, KM, X_LN if m == 0 else None)
                        layer(ch, F_12 + 2 * m + 1, w2, m, hT, KM, None)
                    wait_weights(ch, W_H1)
                    for m in range(KH):
                        layer(ch, F_H1 + m, h1, m, ga, KH, X_12 if m == 0 else None)
                    if not ch.last():
                        turn(ch.go(1))
                    wait_weights(ch, W_H2)
                    for m in range(KH):
                        layer(ch, F_H2 + m, h2, m, gb, KH, X_H1 if m == 0 else None)
                    wait_weights(ch, W_3)
                    for i in range(2):
                        b = job(ch, F_3 + i)[0]
                        wait_free(pe, ch, F_3 + i)
                        for s in range(2):
                            tok = slice((2 * i + s) * P, (2 * i + s + 1) * P)
                            for k in range(KH):
                                if i == 0 and s == 0:
                                    pe.wait_ge(S["lo"], tile(ch, X_H2 + k) + 1)
                                for half in range(2):
                                    mm = product(bank[b][:, s * DM:(s + 1) * DM], ga[:, half, k, tok], w3[:, k, :],
                                                 k == 0 and half == 0, k == KH - 1 and half == 1)
                        mm.then_inc(fill[b], 1)

                turn(Chunk(0, 0, 0))
                schedule(pe, body)

            odd = pe.value_load(any_odd[:, :])
            with pe.If_ne(odd.val, 0):
                program(False)
            with pe.Else():
                program(True)

        @block.scalar
        def _(act):
            def evacuate(ch, i, j, dst, func, **args):
                b = job(ch, i)[0]
                wait_filled(act, ch, i)
                act.activation(dst, bank[b][:, :], func, **args).then_inc(S["hi"], 1)
                wait(act, S["lo"], tile(ch, j) + 1 - XR)
                act.activation(raw[:, j % XR, :], bank[b][:, :], func, **args).then_inc(drain[b], 1)

            def norm_out(ch):
                q = ch.batch
                for k in range(KM):
                    evacuate(ch, F_LN + k, X_LN + k, hT[:, 0, k, :], ACT.Identity, bias=mod[:, 6 + k, q:q + 1],
                             scale=mod[:, 8 + k, q:q + 1])

            def body(ch):
                def round_product(m):
                    wait_drained(act, ch, F_12 + 2 * m + 1)
                    act.copy(ga[:, 0, m, :], raw[:, (X_12 + m) % XR, :]).then_inc(S["hi"], 1)

                for m in range(KH):
                    i = F_12 + 2 * m
                    if m >= 2:
                        wait_drained(act, ch, i - 3)
                    elif not ch.first():
                        wait_drained(act, ch.go(-1), F_12 + 2 * (KH - 2 + m) + 1)
                    wait_filled(act, ch, i)
                    b = job(ch, i)[0]
                    act.activation(s1[:, m % 2, :], bank[b][:, :], ACT.Silu, scale=fcol[:, 0, m:m + 1]).then_inc(drain[b], 1)
                    if m:
                        round_product(m - 1)
                round_product(KH - 1)
                for m in range(KH):
                    evacuate(ch, F_H1 + m, X_H1 + m, gb[:, 0, m, :], ACT.Gelu, scale=fcol[:, 2, m:m + 1])
                if not ch.last():
                    norm_out(ch.go(1))
                for m in range(KH):
                    evacuate(ch, F_H2 + m, X_H2 + m, ga[:, 0, m, :], ACT.Gelu, scale=fcol[:, 3, m:m + 1])

            norm_out(Chunk(0, 0, 0))
            schedule(act, body)

        @block.gpsimd
        def _(pool):
            def norm(ch):
                pool.wait_ge(S["ln"], ch.at(FLN, 2))
                pool.tensor_tensor(mv[:, :, 3], mv[:, :, 1], norm_c[:, 0, :], ALU.add).then_inc(S["ln"], 1)
                pool.wait_ge(S["ln"], ch.at(FLN, 3))
                pool.tensor_tensor(mv[:, :, 2], mv[:, :, 3], norm_c[:, 1, :], ALU.pow).then_inc(S["ln"], 1)

            schedule(pool, norm)

        @block.vector
        def _(dve):
            def norm(ch):
                q = ch.batch
                dve.wait_ge(S[f"x_in{q}"], ch.step * 16 + 16)
                wait(dve, S["ln"], ch.at(FLN, -1))
                for s in range(TS):
                    ins = dve.bn_stats(stat[:, s, :], x1[:, q, s, :])
                ins.then_inc(S["ln"], 1)
                dve.wait_ge(S["ln"], ch.at(FLN, 1))
                dve.sem_inc(S["go"], 1)
                for s in range(TS):
                    ins = dve.bn_aggr(mv[:, s, 0:2], stat[:, s, :])
                ins.then_inc(S["ln"], 1)
                dve.wait_ge(S["ln"], ch.at(FLN, 4))
                if not ch.first():
                    for k in range(KM):
                        wait_filled(dve, ch.go(-1), F_LN + k)
                for s in range(TS):
                    ins = dve.tensor_scalar(xn[:, s, :], x1[:, q, s, :], mv[:, s, 0:1], mv[:, s, 2:3],
                                            ALU.subtract, ALU.mult)
                ins.then_inc(S["ln"], 1)

            def rest(ch, j, i, dst):
                dve.wait_ge(S["hi"], tile(ch, j) + 1)
                wait_drained(dve, ch, i)
                dve.tensor_tensor(dst[:, 1], raw[:, j % XR, :], dst[:, 0].bitcast(F32), ALU.subtract).then_inc(S["lo"], 1)

            def norm_rest(ch):
                for k in range(KM):
                    rest(ch, X_LN + k, F_LN + k, hT[:, :, k, :])

            def body(ch):
                q = ch.batch
                for m in range(KH + 1):
                    if m < KH:
                        i = F_12 + 2 * m
                        b = job(ch, i + 1)[0]
                        wait_drained(dve, ch, i)
                        wait_filled(dve, ch, i + 1)
                        wait(dve, S["lo"], tile(ch, X_12 + m) + 1 - XR)
                        dve.scalar_tensor_tensor(out=raw[:, (X_12 + m) % XR, :], in0=bank[b][:, :],
                                                 scalar=fcol[:, 1, m:m + 1], in1=s1[:, m % 2, :], op0=ALU.mult,
                                                 op1=ALU.mult).then_inc(drain[b], 1)
                    if m:
                        rest(ch, X_12 + m - 1, F_12 + 2 * m - 1, ga[:, :, m - 1, :])
                for m in range(KH):
                    rest(ch, X_H1 + m, F_H1 + m, gb[:, :, m, :])
                    if m == KH // 2 and not ch.last():
                        norm(ch.go(1))
                if not ch.last():
                    norm_rest(ch.go(1))
                for m in range(KH):
                    rest(ch, X_H2 + m, F_H2 + m, ga[:, :, m, :])
                for i in range(2):
                    b = job(ch, F_3 + i)[0]
                    o = ot[:, 2 * i:2 * i + 2, :]
                    wait_filled(dve, ch, F_3 + i)
                    wait(dve, S["o_out"], ch.at(16, 0))
                    dve.tensor_tensor(o, bank[b][:, :].rearrange("p (s n) -> p s n", s=2),
                                      gain[:, 3, q, :].unsqueeze(1).broadcast_to((P, 2, DM)), ALU.mult).then_inc(drain[b], 1)
                    wait_drained(dve, ch, F_3 + i)
                    dve.tensor_tensor(o, o, x1[:, q, 2 * i:2 * i + 2, :], ALU.add).then_inc(S["fin"], 1)

            norm(Chunk(0, 0, 0))
            norm_rest(Chunk(0, 0, 0))
            schedule(dve, body)


def kernel(**inputs):
    import numpy as np
    import concourse.bacc as bacc
    from concourse.bass_utils import run_bass_kernel_spmd

    g = {k: np.asarray(v) for k, v in inputs.items()}
    arrays = {"x": g["L0_attn_x"], "cT": g["L0_c"].T, "wmod": g["L0_wmod"], "ln_g": g["L0_attn_ln_g"],
              "ln_b": g["L0_attn_ln_b"], "w3_s": g["L0_ffn_w3_s"]}

    def by_partition(v):
        return v.reshape(-1, P).T

    for d in "fb":
        m = {n: g[f"L0_attn_{d}_{n}"] for n in ("in_proj", "conv_w", "conv_b", "x_proj", "dt_w", "dt_b", "A_log", "D",
                                                "out_proj")}
        for n in ("in_proj", "x_proj", "dt_w", "out_proj"):
            arrays[f"{d}_{n}T"] = m[n].T
        conv = m["conv_w"].reshape(KI, P, DCONV).transpose(1, 0, 2).reshape(P, -1)
        a_log = m["A_log"].reshape(KI, P, DS).transpose(1, 0, 2).reshape(P, -1)
        arrays[f"{d}_cols"] = np.concatenate([conv, by_partition(m["conv_b"]), by_partition(m["dt_b"]),
                                              by_partition(m["D"]), a_log], axis=1)
    for n in ("w1", "w2", "h1", "h2", "w3"):
        arrays[n + "T"] = g[f"L0_ffn_{n}_w"].T
    arrays["ffn_cols"] = np.stack([by_partition(g[f"L0_ffn_{n}_s"]) for n in ("w1", "w2", "h1", "h2")], axis=1)

    nc = bacc.Bacc("TRN2", target_bir_lowering=False, num_devices=1)
    feeds, aps = {}, {}
    for name, v in arrays.items():
        v = np.ascontiguousarray(v)
        feeds[f"in_{name}"] = v
        aps[name] = nc.dram_tensor(f"in_{name}", v.shape, mybir.dt.from_np(v.dtype), kind="ExternalInput").ap()
    shape = (BATCH, SEQ, DM)
    out = nc.dram_tensor("out", shape, F32, kind="ExternalOutput").ap()
    yb = nc.dram_tensor("yb_dram", shape, F32, kind="Internal").ap()
    x1 = nc.dram_tensor("x1_dram", shape, F32, kind="Internal").ap()
    xn = nc.dram_tensor("xn_dram", shape, F32, kind="Internal").ap()
    b = nc.dram_tensor("b_dram", (BATCH, DS, T), F32, kind="Internal").ap()
    w_raw = {n: nc.dram_tensor(f"raw_{n}", aps[n].shape, F32, kind="Internal").ap()
             for n in FFN_WEIGHTS}
    adaln_mamba_ffn(nc, aps, out, yb, x1, xn, b, w_raw)
    r = run_bass_kernel_spmd(nc, [feeds], core_ids=[0])
    return r.results[0]["out"]
```
